# Optimizing a Trainium2 kernel written in Bass

```python
import numpy as np
import jax
import jax.numpy as jnp

def _softmax(x, axis=-1):
    return jax.nn.softmax(x, axis=axis)

def _gelu(x):
    return jax.nn.gelu(x, approximate=True)

def _silu(x):
    return jax.nn.silu(x)

def _sigmoid(x):
    return jax.nn.sigmoid(x)

def _layernorm(x, axis=-1, eps=1e-05):
    m = jnp.mean(x, axis=axis, keepdims=True)
    v = jnp.var(x, axis=axis, keepdims=True)
    return (x - m) / jnp.sqrt(v + eps)

def _scatter_add(tgt, idx, src, axis=0):
    return tgt.at[idx].add(src)

def _segment_sum(src, seg, n):
    return jax.ops.segment_sum(src, seg, n)
kernel_name = 'mk_seq_postln_d1_jaxref_r8_c7cab3'

def setup_inputs(seed: int=0):
    np.random.seed(seed)
    _w = jnp.asarray

    def _L0_attn_setup():
        import jax, jax.numpy as jnp
        import numpy as np
        B, S, D = (2, 256, 512)
        NH, NKV = (32, 8)
        HD = D // NH
        N_REP = NH // NKV
        key = jax.random.key(seed)
        ks = jax.random.split(key, 5)
        scale = 0.02
        return {'x': jax.random.normal(ks[0], (B, S, D), dtype=jnp.float32), 'wq': jax.random.normal(ks[1], (D, NH * HD), dtype=jnp.float32) * scale, 'wk': jax.random.normal(ks[2], (D, NKV * HD), dtype=jnp.float32) * scale, 'wv': jax.random.normal(ks[3], (D, NKV * HD), dtype=jnp.float32) * scale, 'wo': jax.random.normal(ks[4], (NH * HD, D), dtype=jnp.float32) * scale}
    _L0_attn_in = _L0_attn_setup()

    def _L0_ffn_setup():
        import jax, jax.numpy as jnp
        import numpy as np
        DIM = 512
        INTER = 1792
        SPARSITY = 32
        RANK = 16
        key = jax.random.key(seed)
        ks = jax.random.split(key, 5)
        B, T = (32, 1)
        x = jax.random.normal(ks[0], (B, T, DIM), dtype=jnp.float32)
        c1_w = jax.random.normal(ks[1], (RANK, DIM), dtype=jnp.float32) * (1.0 / np.sqrt(DIM))
        c2_w = jax.random.normal(ks[2], (INTER, RANK), dtype=jnp.float32) * (1.0 / np.sqrt(RANK))
        w1 = jax.random.normal(ks[3], (INTER, DIM), dtype=jnp.float32) * (1.0 / np.sqrt(DIM))
        w2t = jax.random.normal(ks[4], (INTER, DIM), dtype=jnp.float32) * (1.0 / np.sqrt(INTER))
        return {'x': x, 'c1_w': c1_w, 'c2_w': c2_w, 'w1': w1, 'w2t': w2t}
    _L0_ffn_in = _L0_ffn_setup()
    _d = {'L0_attn_x': _L0_attn_in['x'], 'L0_attn_wq': _L0_attn_in['wq'], 'L0_attn_wk': _L0_attn_in['wk'], 'L0_attn_wv': _L0_attn_in['wv'], 'L0_attn_wo': _L0_attn_in['wo'], 'L0_ffn_c1_w': _L0_ffn_in['c1_w'], 'L0_ffn_c2_w': _L0_ffn_in['c2_w'], 'L0_ffn_w1': _L0_ffn_in['w1'], 'L0_ffn_w2t': _L0_ffn_in['w2t']}
    _x0 = _d['L0_attn_x']
    _d['L0_attn_x'] = jax.random.normal(jax.random.fold_in(jax.random.key(seed), 1), (4, 512, 512), dtype=_x0.dtype)
    del _x0
    return _d

def reference(L0_attn_x, L0_attn_wq, L0_attn_wk, L0_attn_wv, L0_attn_wo, L0_ffn_c1_w, L0_ffn_c2_w, L0_ffn_w1, L0_ffn_w2t):

    def _L0_attn_ref(x, wq, wk, wv, wo):
        import jax, jax.numpy as jnp
        import numpy as np
        B, S, D = (2, 256, 512)
        NH, NKV = (32, 8)
        HD = D // NH
        N_REP = NH // NKV
        bsz, toks, _ = x.shape
        q = (x @ wq).reshape(bsz, toks, NH, HD)
        k = (x @ wk).reshape(bsz, toks, NKV, HD)
        v = (x @ wv).reshape(bsz, toks, NKV, HD)
        qg = q.reshape(bsz, toks, NKV, N_REP, HD)
        scores = jnp.einsum('bqgrd,bkgd->bgrqk', qg, k) / jnp.sqrt(jnp.asarray(HD, x.dtype))
        attn = jax.nn.softmax(scores.astype(jnp.float32), axis=-1).astype(x.dtype)
        out = jnp.einsum('bgrqk,bkgd->bqgrd', attn, v)
        out = out.reshape(bsz, toks, NH * HD)
        return out @ wo

    def _L0_ffn_ref(x, c1_w, c2_w, w1, w2t):
        import jax, jax.numpy as jnp
        import numpy as np
        DIM = 512
        INTER = 1792
        SPARSITY = 32
        RANK = 16
        B, T, M = x.shape
        xf = x.reshape(B * T, M)
        inter = xf @ c1_w.T @ c2_w.T
        n_blocks = INTER // SPARSITY
        blk = inter.reshape(B * T, n_blocks, SPARSITY)
        idx = jnp.argmax(blk, axis=-1) + jnp.arange(0, INTER, SPARSITY)
        w1_g = w1[idx]
        w2_g = w2t[idx]
        h = jax.nn.relu(jnp.einsum('bkm,bm->bk', w1_g, xf))
        out = jnp.einsum('bk,bkm->bm', h, w2_g)
        return out.reshape(B, T, M)
    x = L0_attn_x
    x = _layernorm(x + _L0_attn_ref(x, L0_attn_wq, L0_attn_wk, L0_attn_wv, L0_attn_wo), axis=-1)
    x = _layernorm(x + _L0_ffn_ref(x, L0_ffn_c1_w, L0_ffn_c2_w, L0_ffn_w1, L0_ffn_w2t), axis=-1)
    return x

_drawn_inputs = setup_inputs


def setup_inputs(seed=0):
    import zlib

    import numpy as np

    out = dict(_drawn_inputs(seed))
    spreads = {}
    factors = {'L0_attn_wq': 6.906, 'L0_attn_wk': 6.764, 'L0_attn_wv': 3.314, 'L0_attn_wo': 3.225}
    for name, (base, spread) in spreads.items():
        noise = np.random.default_rng([zlib.crc32(name.encode()), seed]).standard_normal(out[name].shape)
        drawn = base * np.exp(spread * noise) if base else spread * noise
        out[name] = jnp.asarray(drawn.astype(out[name].dtype))
    for name, factor in factors.items():
        out[name] = (out[name] * factor).astype(out[name].dtype)
    return out
```

```python
import concourse.bass as bass
from concourse import mybir
from contextlib import ExitStack

F32 = mybir.dt.float32
F32R = mybir.dt.float32r
BF16 = mybir.dt.bfloat16
ALU = mybir.AluOpType
ACT = mybir.ActivationFunctionType
AX = mybir.AxisListType

P = 128
NB = 4
S = 512
D = 512
NH, NKV = 32, 8
HD = D // NH
REP = NH // NKV
KT = D // P
TT = S // P
KV = NKV * HD
INTER, BLK, RANK = 1792, 32, 16
MT = INTER // P
CH = 448
NC = INTER // CH
EPS = 1e-5
DMA = 16

STACK = 3 * HD
SHIFT = STACK
ROWS = STACK + 2
Q_UNIT = 2 * STACK * 2 * S
K_UNIT = STACK * S
V_UNIT = P * TT * 2 * HD
N_UNIT = REP * HD * S
VW = 2 * HD


def _scratch(nc, name, n):
    return nc.dram_tensor(name, (n,), F32, kind="Internal").ap()


def _project(nc, xT, w_qkv, qs, ks, vs, wo, c1, c2, keep):
    WQ = D + 2 * KV
    wo_h, wo_l, c1_h, c1_l, c2_s = keep
    with ExitStack() as ctx:
        sb = lambda name, shape, dt: ctx.enter_context(nc.sbuf_tensor(name, shape, dt))
        sem = lambda name: ctx.enter_context(nc.semaphore(name))
        w_raw = sb("w_raw", [P, KT, WQ], F32)
        w_h = sb("w_h", [P, KT, WQ], F32R)
        w_l = sb("w_l", [P, KT, WQ], F32R)
        x_raw = [sb(f"x_raw{j}", [P, KT, S], F32) for j in range(2)]
        x_h = [sb(f"x_h{j}", [P, KT, S], F32R) for j in range(2)]
        x_l = [sb(f"x_l{j}", [P, KT, S], F32R) for j in range(2)]
        p_h = [[sb(f"p_h{j}_{s}", [P, S], F32R) for s in range(REP + 1)] for j in range(2)]
        p_l = [[sb(f"p_l{j}_{s}", [P, S], F32R) for s in range(REP + 1)] for j in range(2)]
        v_sb = [sb(f"v_sb{j}", [P, TT, NKV, VW], F32) for j in range(2)]
        wo_raw = sb("wo_raw", [P, REP, D], F32)
        c1_raw = sb("c1_raw", [P, KT, 80], F32)
        c2_raw = sb("c2_raw", [80, INTER], F32)
        bank = [ctx.enter_context(nc.psum_tensor(f"proj{s}", [P, 512], F32)) for s in range(6)]

        w_in = [sem(f"w_in{k}") for k in range(KT)]
        w_high, w_split = sem("w_high"), sem("w_split")
        x_in = [sem(f"x_in{j}") for j in range(2)]
        x_high, x_split = sem("x_high"), sem("x_split")
        projected = sem("projected")
        high_out, evacuated = sem("high_out"), sem("evacuated")
        v_ones = sem("v_ones")
        stored = [sem(f"stored{j}") for j in range(2)]
        pre_in, pre_zero, pre = sem("pre_in"), sem("pre_zero"), sem("pre")
        GROUPS = REP + 2
        STORES = 3 * REP + 3 + 1

        x_v = xT.rearrange("(k p) t -> p k t", p=P)
        w_v = w_qkv.rearrange("(k p) n -> p k n", p=P)
        block = ctx.enter_context(nc.Block())

        @block.sync
        def _(sp):
            def load_x(b):
                if b >= 2:
                    sp.wait_ge(x_split, b - 1)
                sp.dma_start(x_raw[b % 2][:], x_v[:, :, b * S:(b + 1) * S]).then_inc(x_in[b % 2], DMA)
            load_x(0)
            for k in range(KT):
                sp.dma_start(w_raw[:, k], w_v[:, k]).then_inc(w_in[k], DMA)
            load_x(1)
            for b in range(NB):
                if b + 2 < NB:
                    load_x(b + 2)
                for s in range(REP + 1):
                    sp.wait_ge(evacuated, GROUPS * b + s + 1)
                    h, l = p_h[b % 2][s][:].bitcast(F32), p_l[b % 2][s][:].bitcast(F32)
                    if s < REP:
                        parts = (h, h, l)
                        dst = qs[b * NKV * Q_UNIT:(b + 1) * NKV * Q_UNIT].rearrange(
                            "(g a s d j t) -> a s j g d t", g=NKV, a=2, s=3, d=HD, j=2)
                        dst = [dst[s % 2, n, s // 2] for n in range(3)]
                    else:
                        parts = (h, l, h)
                        dst = ks[b * NKV * K_UNIT:(b + 1) * NKV * K_UNIT].rearrange(
                            "(g s d t) -> s g d t", g=NKV, s=3, d=HD)
                        dst = [dst[n] for n in range(3)]
                    for n in range(3):
                        sp.dma_start(dst[n], parts[n]).then_inc(stored[b % 2], DMA)
                sp.wait_ge(evacuated, GROUPS * (b + 1))
                dst = vs[b * NKV * V_UNIT:(b + 1) * NKV * V_UNIT].rearrange(
                    "(g p k c) -> p k g c", g=NKV, p=P, k=TT)
                for k in range(TT):
                    sp.dma_start(dst[:, k], v_sb[b % 2][:, k]).then_inc(stored[b % 2], DMA)
            for j in range(2):
                sp.wait_ge(stored[j], (NB // 2) * (STORES + 3) * DMA)

        @block.gpsimd
        def _(pool):
            nc.gpsimd.memset(c1_raw[:], 0.0).then_inc(pre_zero, 1)
            nc.gpsimd.memset(c2_raw[:], 0.0).then_inc(pre_zero, 1)
            pool.dma_start(wo_raw[:], wo.rearrange("(r p) n -> p r n", p=P)).then_inc(pre_in, DMA)
            pool.wait_ge(pre_zero, 2)
            for n in range(3):
                pool.dma_start(c1_raw[:, :, 32 * n:32 * n + RANK],
                               c1.rearrange("(k p) n -> p k n", p=P)).then_inc(pre_in, DMA)
                pool.dma_start(c2_raw[32 * n:32 * n + RANK, :], c2).then_inc(pre_in, DMA)
            pool.wait_ge(pre_in, 7 * DMA)
            nc.gpsimd.tensor_copy(wo_h[:], wo_raw[:]).then_inc(pre, 1)
            nc.gpsimd.tensor_copy(c1_h[:], c1_raw[:]).then_inc(pre, 1)
            nc.gpsimd.tensor_copy(c2_s[:], c2_raw[:]).then_inc(pre, 1)
            pool.wait_ge(pre, 3)
            nc.gpsimd.tensor_tensor(wo_l[:], wo_raw[:], wo_h[:].bitcast(F32), ALU.subtract).then_inc(pre, 1)
            nc.gpsimd.tensor_tensor(c1_l[:], c1_raw[:], c1_h[:].bitcast(F32), ALU.subtract).then_inc(pre, 1)
            pool.wait_ge(pre, 5)
            nc.gpsimd.tensor_tensor(c2_s[64:80], c2_raw[64:80], c2_s[64:80].bitcast(F32),
                                    ALU.subtract).then_inc(pre, 1)

        @block.scalar
        def _(act):
            def high_x(b):
                act.wait_ge(x_in[b % 2], DMA * (b // 2 + 1))
                if b >= 2:
                    act.wait_ge(projected, GROUPS * (b - 1))
                nc.scalar.activation(x_h[b % 2][:], x_raw[b % 2][:], ACT.Copy).then_inc(x_high, 1)
            high_x(0)
            for k in range(KT):
                act.wait_ge(w_in[k], DMA)
                nc.scalar.activation(w_h[:, k], w_raw[:, k], ACT.Copy).then_inc(w_high, 1)
            high_x(1)
            for b in range(NB):
                if b >= 2:
                    act.wait_ge(stored[b % 2], (b // 2) * (STORES + 3) * DMA)
                for s in range(REP + 1):
                    act.wait_ge(projected, GROUPS * b + s + 1)
                    nc.scalar.activation(p_h[b % 2][s][:], bank[s][:], ACT.Copy).then_inc(high_out, 1)
                if b + 2 < NB:
                    high_x(b + 2)

        @block.vector
        def _(dve):
            for j in range(2):
                nc.vector.memset(v_sb[j][:, :, :, HD:VW], 1.0).then_inc(v_ones, 1)

            def low_x(b):
                dve.wait_ge(x_high, b + 1)
                nc.vector.tensor_tensor(x_l[b % 2][:], x_raw[b % 2][:], x_h[b % 2][:].bitcast(F32),
                                        ALU.subtract).then_inc(x_split, 1)
            low_x(0)
            for k in range(KT):
                dve.wait_ge(w_high, k + 1)
                nc.vector.tensor_tensor(w_l[:, k], w_raw[:, k], w_h[:, k].bitcast(F32),
                                        ALU.subtract).then_inc(w_split, 1)
            low_x(1)
            for b in range(NB):
                for s in range(REP + 1):
                    dve.wait_ge(high_out, (REP + 1) * b + s + 1)
                    nc.vector.tensor_tensor(p_l[b % 2][s][:], bank[s][:], p_h[b % 2][s][:].bitcast(F32),
                                            ALU.subtract).then_inc(evacuated, 1)
                dve.wait_ge(projected, GROUPS * (b + 1))
                if b < 2:
                    dve.wait_ge(v_ones, b + 1)
                else:
                    dve.wait_ge(stored[b % 2], (b // 2) * (STORES + 3) * DMA)
                nc.vector.tensor_copy(v_sb[b % 2][:, :, :, 0:HD],
                                      bank[5][:].rearrange("p (k g d) -> p k g d", k=TT, g=NKV)
                                      ).then_inc(evacuated, 1)
                if b + 2 < NB:
                    low_x(b + 2)

        @block.tensor
        def _(pe):
            for b in range(NB):
                pe.wait_ge(x_split, b + 1)
                xs = (x_h[b % 2], x_h[b % 2], x_l[b % 2])
                ws = (w_h, w_l, w_h)
                for s in range(REP + 1):
                    if b:
                        pe.wait_ge(evacuated, GROUPS * (b - 1) + s + 1)
                    for k in range(KT):
                        if b == 0 and s == 0:
                            pe.wait_ge(w_split, k + 1)
                        for n in range(3):
                            last = nc.tensor.matmul(bank[s][:], ws[n][:, k, s * P:(s + 1) * P], xs[n][:, k],
                                                    start=(k == 0 and n == 0), stop=(k == KT - 1 and n == 2))
                    last.then_inc(projected, 1)
                if b:
                    pe.wait_ge(evacuated, GROUPS * b)
                for t in range(TT):
                    for k in range(KT):
                        for n in range(3):
                            last = nc.tensor.matmul(bank[5][:, t * KV:(t + 1) * KV],
                                                    xs[n][:, k, t * P:(t + 1) * P], ws[n][:, k, D + KV:],
                                                    start=(k == 0 and n == 0), stop=(k == KT - 1 and n == 2))
                last.then_inc(projected, 1)


def _attend(nc, x, qs, ks, vs, num, den, rden, x1, wo_h, wo_l, w1, w1_h, w1_l, ident):
    NU = NB * NKV
    QR = 4
    with ExitStack() as ctx:
        sb = lambda name, shape, dt: ctx.enter_context(nc.sbuf_tensor(name, shape, dt))
        sem = lambda name: ctx.enter_context(nc.semaphore(name))
        ps = lambda name, shape: ctx.enter_context(nc.psum_tensor(name, shape, F32))
        q = [sb(f"q{j}", [P, 2, S], F32R) for j in range(QR)]
        k_ = [sb(f"k{j}", [P, S], F32R) for j in range(QR)]
        v = [sb(f"v{j}", [P, TT, VW], F32) for j in range(QR)]
        probs = [sb(f"probs{j}", [P, REP, S], F32) for j in range(4)]
        neg_max = sb("neg_max", [P, TT, 2, 2], F32)
        max_parts = sb("max_parts", [P, TT, 2, 2, 2], F32R)
        shift = [sb(f"shift{j}", [8, S], F32R) for j in range(2)]
        stage = [sb(f"stage{j}", [P, S], F32) for j in range(2)]
        att = sb("att", [P, REP, S], F32)
        att_h = sb("att_h", [P, REP, S], F32R)
        att_l = sb("att_l", [P, REP, S], F32R)
        rb = sb("rb", [P, REP, S], F32)
        den_sb = sb("den_sb", [P, P], F32)
        rden_sb = sb("rden_sb", [P, P], F32)
        x_sb = [sb(f"x_sb{j}", [P, D], F32) for j in range(2)]
        y = sb("y", [P, TT, D], F32)
        stats = sb("stats", [P, TT, 6], F32)
        mv = sb("mv", [P, TT, 2], F32)
        var = sb("var", [P, TT], F32)
        rstd = sb("rstd", [P, TT], F32)
        neg_half = sb("neg_half", [P, TT], F32)
        w1_raw = [sb(f"w1_raw{j}", [P, CH], F32) for j in range(2)]
        ps_max = [ps(f"ps_max{j}", [P, 2, S]) for j in range(2)]
        ps_st = [ps(f"ps_st{j}", [P, S]) for j in range(2)]
        ps_pv = ps("ps_pv", [P, S])
        ps_x = ps("ps_x", [P, S])

        k_ones = sem("k_ones")
        unit_in = [sem(f"unit_in{j}") for j in range(QR)]
        max_mm, max_red = sem("max_mm"), sem("max_red")
        max_high, max_split, max_turned, shift_ready = (sem("max_high"), sem("max_split"),
                                                        sem("max_turned"), sem("shift_ready"))
        shift_in = [sem(f"shift_in{j}") for j in range(QR)]
        st_mm, exp_done, pv_done, stage_ready = sem("st_mm"), sem("exp_done"), sem("pv_done"), sem("stage_ready")
        num_out = [sem(f"num_out{j}") for j in range(2)]
        att_in, den_in, rden_ready, rden_out, rb_in = (sem("att_in"), sem("den_in"), sem("rden_ready"),
                                                       sem("rden_out"), sem("rb_in"))
        att_step, att_ready = sem("att_step"), sem("att_ready")
        wo_done, x_in, y_ready = sem("wo_done"), [sem("xr_in0"), sem("xr_in1")], sem("y_ready")
        stat_done, aggr_done, var_ready, rstd_ready = (sem("stat_done"), sem("aggr_done"),
                                                       sem("var_ready"), sem("rstd_ready"))
        half_set = sem("half_set")
        x1_ready, x1_out = sem("x1_ready"), sem("x1_out")
        w1_in, w1_high, w1_low = [sem("w1_in0"), sem("w1_in1")], sem("w1_high"), sem("w1_low")
        LOADS, STORES = 5, 5
        WO_AT = (3, 4, 5, 6)
        block = ctx.enter_context(nc.Block())

        @block.sync
        def _(sp):
            def load_unit(n):
                j = n % QR
                if n >= QR:
                    sp.wait_ge(pv_done, TT * (n - QR + 1))
                else:
                    sp.wait_ge(k_ones, 2 * QR)
                for a in range(2):
                    at = n * Q_UNIT + a * STACK * 2 * S
                    sp.dma_start(q[j][64 * a:64 * a + STACK].bitcast(F32),
                                 qs[at:at + STACK * 2 * S].rearrange("(s j t) -> s j t", s=STACK, j=2)
                                 ).then_inc(unit_in[j], DMA)
                    sp.dma_start(k_[j][64 * a:64 * a + STACK].bitcast(F32),
                                 ks[n * K_UNIT:(n + 1) * K_UNIT].rearrange("(s t) -> s t", t=S)
                                 ).then_inc(unit_in[j], DMA)
                sp.dma_start(v[j][:], vs[n * V_UNIT:(n + 1) * V_UNIT].rearrange("(p k c) -> p k c", p=P, k=TT)
                             ).then_inc(unit_in[j], DMA)

            def store_unit(n):
                b, g = n // NKV, n % NKV
                sp.wait_ge(stage_ready, n + 1)
                for r in range(REP):
                    at = ((b * REP + r) * NKV + g) * HD * S
                    sp.dma_start(num[at:at + HD * S].rearrange("(d t) -> d t", d=HD),
                                 stage[n % 2][32 * r:32 * r + HD]).then_inc(num_out[n % 2], DMA)
                at = n * REP * S
                sp.dma_start(den[at:at + REP * S].rearrange("(r t) -> r t", r=REP),
                             stage[n % 2][HD:HD + 32 * (REP - 1) + 1:32]).then_inc(num_out[n % 2], DMA)

            def send_shift(n):
                sp.wait_ge(shift_ready, n + 1)
                for a in range(2):
                    sp.dma_start(q[n % QR][64 * a + SHIFT:64 * a + SHIFT + 2].bitcast(F32),
                                 shift[n % 2][4 * a:4 * a + 4].bitcast(F32)
                                 ).then_inc(shift_in[n % QR], DMA)

            def load_x(b, t):
                i = b * TT + t
                if i >= 2:
                    sp.wait_ge(y_ready, i - 1)
                sp.dma_start(x_sb[i % 2][:], x[(b * TT + t) * P:(b * TT + t + 1) * P]).then_inc(x_in[i % 2], DMA)

            def store_x1(b):
                sp.wait_ge(x1_ready, TT * (b + 1))
                sp.dma_start(x1[b * S * D:(b + 1) * S * D].rearrange("(t p d) -> p t d", t=TT, p=P),
                             y[:]).then_inc(x1_out, DMA)

            for n in range(3):
                load_unit(n)
            send_shift(0)
            for b in range(NB):
                for g in range(NKV):
                    n = b * NKV + g
                    if n:
                        store_unit(n - 1)
                    if n + 3 < NU:
                        load_unit(n + 3)
                    if n + 1 < NU:
                        send_shift(n + 1)
                    if b and g + 1 in WO_AT:
                        load_x(b - 1, g + 1 - WO_AT[0])
                if b:
                    store_x1(b - 1)
            store_unit(NU - 1)
            for t in range(TT):
                load_x(NB - 1, t)
            store_x1(NB - 1)
            sp.wait_ge(x1_out, NB * DMA)

        @block.gpsimd
        def _(pool):
            nc.gpsimd.memset(neg_half[:], -0.5).then_inc(half_set, 1)
            w1_v = w1.rearrange("(k p) n -> p k n", p=P)

            def load_w1(i):
                if i >= 2:
                    pool.wait_ge(w1_low, i - 1)
                pool.dma_start(w1_raw[i % 2][:], w1_v[:, i // NC, (i % NC) * CH:(i % NC + 1) * CH]
                               ).then_inc(w1_in[i % 2], DMA)
            load_w1(0)
            for i in range(KT * NC):
                if i + 1 < KT * NC:
                    load_w1(i + 1)
                k, c = i // NC, i % NC
                pool.wait_ge(w1_in[i % 2], DMA * (i // 2 + 1))
                nc.gpsimd.tensor_copy(w1_h[:, k, c * CH:(c + 1) * CH], w1_raw[i % 2][:]).then_inc(w1_high, 1)
                pool.wait_ge(w1_high, i + 1)
                nc.gpsimd.tensor_tensor(w1_l[:, k, c * CH:(c + 1) * CH], w1_raw[i % 2][:],
                                        w1_h[:, k, c * CH:(c + 1) * CH].bitcast(F32),
                                        ALU.subtract).then_inc(w1_low, 1)
            for b in range(NB):
                for j in range(2):
                    pool.wait_ge(num_out[j], (b + 1) * (NKV // 2) * STORES * DMA)
                if b:
                    pool.wait_ge(att_step, 3 * b)
                pool.dma_start(den_sb[:], den[b * NH * S:(b + 1) * NH * S].rearrange("(p t) -> p t", p=P)
                               ).then_inc(den_in, DMA)
                pool.dma_start(att[:], num[b * NH * HD * S:(b + 1) * NH * HD * S].rearrange(
                    "(r p t) -> p r t", r=REP, p=P)).then_inc(att_in, DMA)
                pool.wait_ge(rden_ready, b + 1)
                pool.dma_start(rden[b * NH * S:(b + 1) * NH * S].rearrange("(p t) -> p t", p=P),
                               rden_sb[:]).then_inc(rden_out, DMA)
                pool.wait_ge(rden_out, DMA * (b + 1))
                for g in range(NKV):
                    at = (b * NKV + g) * REP * S
                    pool.dma_start(rb[HD * g:HD * (g + 1)].rearrange("p r t -> p (r t)"),
                                   rden[at:at + REP * S].rearrange("(o t) -> o t", o=1).broadcast_to([HD, REP * S])
                                   ).then_inc(rb_in, DMA)
                pool.wait_ge(att_in, DMA * (b + 1))
                pool.wait_ge(rb_in, DMA * NKV * (b + 1))
                nc.gpsimd.tensor_tensor(att[:], att[:], rb[:], ALU.mult).then_inc(att_step, 1)
                pool.wait_ge(att_step, 3 * b + 1)
                if b:
                    pool.wait_ge(wo_done, TT * b)
                nc.gpsimd.tensor_copy(att_h[:], att[:]).then_inc(att_step, 1)
                pool.wait_ge(att_step, 3 * b + 2)
                nc.gpsimd.tensor_tensor(att_l[:], att[:], att_h[:].bitcast(F32), ALU.subtract
                                        ).then_inc(att_step, 1)
                pool.wait_ge(var_ready, b + 1)
                if b == 0:
                    pool.wait_ge(half_set, 1)
                nc.gpsimd.tensor_tensor(rstd[:], var[:], neg_half[:], ALU.pow).then_inc(rstd_ready, 1)

        @block.scalar
        def _(act):
            def turn_shift(n):
                act.wait_ge(max_turned, n + 1)
                if n >= 2:
                    act.wait_ge(shift_in[(n - 2) % QR], 2 * DMA * ((n - 2) // QR + 1))
                nc.scalar.activation(shift[n % 2][:], ps_x[0:8], ACT.Copy).then_inc(shift_ready, 1)

            def take_sums(n):
                act.wait_ge(pv_done, TT * (n + 1))
                if n >= 2:
                    act.wait_ge(num_out[n % 2], STORES * DMA * (n // 2))
                nc.scalar.activation(stage[n % 2][:], ps_pv[:], ACT.Copy).then_inc(stage_ready, 1)

            turn_shift(0)
            for n in range(NU):
                for kt in range(TT):
                    for r in range(REP):
                        i = (n * TT + kt) * REP + r
                        act.wait_ge(st_mm, i + 1)
                        if r == 0 and n * TT + kt >= 4:
                            act.wait_ge(pv_done, n * TT + kt - 3)
                        nc.scalar.activation(probs[kt][:, r], ps_st[r % 2][:], ACT.Exp,
                                             scale=float(HD) ** -0.5).then_inc(exp_done, 1)
                    if kt == 0:
                        if n:
                            take_sums(n - 1)
                        if n + 1 < NU:
                            turn_shift(n + 1)
            take_sums(NU - 1)

        @block.vector
        def _(dve):
            def row_max(n, i):
                dve.wait_ge(max_mm, 8 * n + i + 1)
                if n and i == 0:
                    dve.wait_ge(max_split, n)
                nc.vector.tensor_reduce(neg_max[:, i // 2, :, i % 2], ps_max[i % 2][:], AX.X, ALU.max,
                                        negate=True).then_inc(max_red, 1)

            def split_max(n):
                dve.wait_ge(max_red, 8 * (n + 1))
                if n:
                    dve.wait_ge(max_turned, n)
                nc.vector.tensor_copy(max_parts[:, :, :, 0], neg_max[:]).then_inc(max_high, 1)
                dve.wait_ge(max_high, n + 1)
                nc.vector.tensor_tensor(max_parts[:, :, :, 1], neg_max[:], max_parts[:, :, :, 0].bitcast(F32),
                                        ALU.subtract).then_inc(max_split, 1)

            def recip(b):
                dve.wait_ge(den_in, DMA * (b + 1))
                if b:
                    dve.wait_ge(rden_out, DMA * b)
                nc.vector.reciprocal(rden_sb[:], den_sb[:]).then_inc(rden_ready, 1)

            def add_tile(b, t):
                i = b * TT + t
                dve.wait_ge(wo_done, i + 1)
                dve.wait_ge(x_in[i % 2], DMA * (i // 2 + 1))
                if b:
                    dve.wait_ge(x1_out, DMA * b)
                nc.vector.tensor_tensor(y[:, t], ps_x[:], x_sb[i % 2][:], ALU.add).then_inc(y_ready, 1)
                dve.wait_ge(y_ready, i + 1)
                nc.vector.bn_stats(stats[:, t], y[:, t]).then_inc(stat_done, 1)
                dve.wait_ge(stat_done, i + 1)
                nc.vector.bn_aggr(mv[:, t], stats[:, t]).then_inc(aggr_done, 1)

            def norm_ready(b):
                dve.wait_ge(aggr_done, TT * (b + 1))
                if b:
                    dve.wait_ge(rstd_ready, b)
                nc.vector.tensor_scalar(var[:], mv[:, :, 1], EPS, None, ALU.add).then_inc(var_ready, 1)

            def norm(b):
                dve.wait_ge(rstd_ready, b + 1)
                for t in range(TT):
                    nc.vector.tensor_scalar(y[:, t], y[:, t], mv[:, t, 0:1], rstd[:, t:t + 1],
                                            ALU.subtract, ALU.mult).then_inc(x1_ready, 1)

            for j in range(QR):
                for a in range(2):
                    nc.vector.memset(k_[j][64 * a + 32:64 * a + 64].bitcast(F32), 1.0).then_inc(k_ones, 1)
            for n in range(2):
                for i in range(8):
                    row_max(n, i)
                split_max(n)
            for b in range(NB):
                for g in range(NKV):
                    n = b * NKV + g
                    if n + 2 < NU:
                        for i in range(8):
                            row_max(n + 2, i)
                            if i == 6 and b and g in WO_AT:
                                add_tile(b - 1, g - WO_AT[0])
                        split_max(n + 2)
                    elif b and g in WO_AT:
                        add_tile(b - 1, g - WO_AT[0])
                    if b and g == 0:
                        recip(b - 1)
                    if b and g == WO_AT[-1]:
                        norm_ready(b - 1)
                    if b and g == NKV - 1:
                        norm(b - 1)
            recip(NB - 1)
            for t in range(TT):
                add_tile(NB - 1, t)
            norm_ready(NB - 1)
            norm(NB - 1)

        @block.tensor
        def _(pe):
            def scores(n, i):
                if i == 0:
                    pe.wait_ge(unit_in[n % QR], LOADS * DMA * (n // QR + 1))
                if 8 * n + i >= 2:
                    pe.wait_ge(max_red, 8 * n + i - 1)
                t, j = i // 2, i % 2
                for a in range(2):
                    last = nc.tensor.matmul(ps_max[i % 2][:, a],
                                            q[n % QR][64 * a:64 * a + STACK, j, t * P:(t + 1) * P],
                                            k_[n % QR][64 * a:64 * a + STACK, :], start=True, stop=True)
                last.then_inc(max_mm, 1)

            def turn_max(n):
                pe.wait_ge(max_split, n + 1)
                turned_at = n - 1
                tiles = TT * (turned_at // NKV - 1) + sum(g < turned_at % NKV for g in WO_AT)
                if n and tiles > 0:
                    pe.wait_ge(y_ready, tiles)
                if n >= 1:
                    pe.wait_ge(shift_ready, n)
                for t in range(TT):
                    last = nc.tensor.transpose(ps_x[0:8, t * P:(t + 1) * P],
                                               max_parts[:, t].rearrange("p a h j -> p (a h j)").bitcast(F32), ident[:])
                last.then_inc(max_turned, 1)

            def scores_t(n, kt, r):
                i = (n * TT + kt) * REP + r
                if kt == 0 and r == 0:
                    pe.wait_ge(shift_in[n % QR], 2 * DMA * (n // QR + 1))
                if i >= 2:
                    pe.wait_ge(exp_done, i - 1)
                a, j = r % 2, r // 2
                nc.tensor.matmul(ps_st[r % 2][:], k_[n % QR][64 * a:64 * a + ROWS, kt * P:(kt + 1) * P],
                                 q[n % QR][64 * a:64 * a + ROWS, j, :], start=True, stop=True).then_inc(st_mm, 1)

            def weigh(n, kt):
                pe.wait_ge(exp_done, (n * TT + kt + 1) * REP)
                if kt == 0 and n:
                    pe.wait_ge(stage_ready, n)
                for r in range(REP):
                    last = nc.tensor.matmul(ps_pv[32 * r:32 * r + VW], v[n % QR][:, kt], probs[kt][:, r],
                                            start=(kt == 0), stop=(kt == TT - 1))
                last.then_inc(pv_done, 1)

            def project_out(b, t):
                i = b * TT + t
                if t == 0:
                    pe.wait_ge(att_step, 3 * (b + 1))
                if i:
                    pe.wait_ge(y_ready, i)
                pe.wait_ge(shift_ready, (b + 1) * NKV + WO_AT[t] + 2 if b < NB - 1 else NU)
                for r in range(REP):
                    for n, (a, w) in enumerate(((att_h, wo_h), (att_h, wo_l), (att_l, wo_h))):
                        last = nc.tensor.matmul(ps_x[:], a[:, r, t * P:(t + 1) * P], w[:, r],
                                                start=(r == 0 and n == 0), stop=(r == REP - 1 and n == 2))
                last.then_inc(wo_done, 1)

            for i in range(8):
                scores(0, i)
            turn_max(0)
            for i in range(8):
                scores(1, i)
            for b in range(NB):
                for g in range(NKV):
                    n = b * NKV + g
                    for kt in range(TT):
                        for r in range(REP):
                            scores_t(n, kt, r)
                            if r % 2 and n + 2 < NU:
                                scores(n + 2, 2 * kt + r // 2)
                        if kt:
                            weigh(n, kt - 1)
                        elif n:
                            weigh(n - 1, TT - 1)
                        if kt == 0 and n + 1 < NU:
                            turn_max(n + 1)
                        if kt == 2 and b and g in WO_AT:
                            project_out(b - 1, g - WO_AT[0])
            weigh(NU - 1, TT - 1)
            for t in range(TT):
                project_out(NB - 1, t)


def _feed_forward(nc, x1, out, w2, w1_h, w1_l, c1_h, c1_l, c2_s, ident, ident16, first):
    U = TT
    EARLY = TT + 1 + TT
    marks = lambda c, t: TT + 1 + c * TT + t
    with ExitStack() as ctx:
        sb = lambda name, shape, dt=F32: ctx.enter_context(nc.sbuf_tensor(name, shape, dt))
        sem = lambda name: ctx.enter_context(nc.semaphore(name))
        ps = lambda name, shape, dt=F32: ctx.enter_context(nc.psum_tensor(name, shape, dt))
        w2_h = sb("w2_h", [P, MT, D], F32R)
        w2_l = sb("w2_l", [P, MT, D], F32R)
        w2_raw = [sb(f"w2_raw{j}", [P, D]) for j in range(2)]
        xt_h = [sb(f"xt_h{j}", [P, KT, S], F32R) for j in range(2)]
        xt_l = [sb(f"xt_l{j}", [P, KT, S], F32R) for j in range(2)]
        u = sb("u", [80, S], F32R)
        x_sb = [sb(f"xf_sb{j}", [P, D]) for j in range(2)]
        top = [sb(f"top{j}", [P, CH // BLK]) for j in range(2)]
        mask = sb("mask", [P, TT, INTER], BF16)
        mask_t = [sb(f"mask_t{j}", [P, S], BF16) for j in range(2)]
        act_r = [sb(f"relu{j}", [P, S]) for j in range(2)]
        picked = [sb(f"picked{j}", [P, S]) for j in range(2)]
        g_h = [sb(f"g_h{j}", [P, S], F32R) for j in range(2)]
        g_l = [sb(f"g_l{j}", [P, S], F32R) for j in range(2)]
        y = sb("yf", [P, TT, D])
        stats = sb("statsf", [P, TT, 6])
        mv = sb("mvf", [P, TT, 2])
        var = sb("varf", [P, TT])
        rstd = sb("rstdf", [P, TT])
        neg_half = sb("neg_halff", [P, TT])
        ps_out = [ps(f"ps_out{t}", [P, D]) for t in range(TT)]
        ps_h, ps_z, ps_prep = ps("ps_h", [P, S]), ps("ps_z", [P, S]), ps("ps_prep", [P, S])
        ps_t = ps("ps_t", [P, S], BF16)

        x_in = [sem(f"xf_in{j}") for j in range(2)]
        prep_mm, prep_half, prep_done = sem("prep_mm"), sem("prep_half"), sem("prep_done")
        mask_turned, mask_t_ready = sem("mask_turned"), sem("mask_t_ready")
        h_done, relu_ready, z_done, picked_ready = (sem("h_done"), sem("relu_ready"), sem("z_done"),
                                                    sem("picked_ready"))
        g_high, g_ready, out_mm = sem("g_high"), sem("g_ready"), sem("out_mm")
        w2_in, w2_high, w2_low = [sem("w2_in0"), sem("w2_in1")], sem("w2_high"), sem("w2_low")
        y_in, y_ready, stat_done, aggr_done = sem("yf_in"), sem("yf_ready"), sem("statf_done"), sem("aggrf_done")
        half_set, var_ready, rstd_ready = sem("halff_set"), sem("varf_ready"), sem("rstdf_ready")
        out_ready, out_sent = sem("out_ready"), sem("out_sent")
        block = ctx.enter_context(nc.Block())

        def slot_steps(m, last):
            own = {0: ((1, 0), (1, 1)), 1: ((1, 2), (1, 3)), 2: ((2, 0),), 3: ((2, 1),), 4: ((2, 2),),
                   5: ((2, 3),), 6: ((3, 0), (3, 1)), 7: ((3, 2), (3, 3))}
            ahead = {2: (0,), 3: (1,), 4: (2,), 5: (3,), 8: (U,), 9: (marks(0, 0),), 10: (marks(0, 1),),
                     11: (marks(0, 2),), 12: (marks(0, 3),)}
            return ([(0, marks(c, t)) for c, t in own.get(m, ())]
                    + [(1, s) for s in (() if last else ahead.get(m, ()))])

        def number(b, s):
            if b == 0 and s < EARLY:
                return s
            at, key = (b - 1, (1, s)) if s < EARLY else (b, (0, s))
            steps = [k for m in range(MT) for k in slot_steps(m, at == NB - 1)]
            return EARLY + at * len([k for m in range(MT) for k in slot_steps(m, False)]) + steps.index(key)

        @block.sync
        def _(sp):
            def load_x(b, t):
                i = b * TT + t
                if i >= 2:
                    bb, tt = divmod(i - 2, TT)
                    sp.wait_ge(prep_mm, number(bb, tt) + 1)
                sp.dma_start(x_sb[t % 2][:], x1[i * P * D:(i + 1) * P * D].rearrange("(p d) -> p d", p=P)
                             ).then_inc(x_in[t % 2], DMA)

            def load_w2(m):
                if m >= 2:
                    sp.wait_ge(w2_low, m - 1)
                sp.dma_start(w2_raw[m % 2][:], w2[m * P:(m + 1) * P]).then_inc(w2_in[m % 2], DMA)

            def load_y(b):
                if b:
                    sp.wait_ge(out_sent, DMA * b)
                sp.dma_start(y[:], x1[b * S * D:(b + 1) * S * D].rearrange("(t p d) -> p t d", t=TT, p=P)
                             ).then_inc(y_in, DMA)

            def store(b):
                sp.wait_ge(out_ready, TT * (b + 1))
                sp.dma_start(out[b * S:(b + 1) * S].rearrange("(t p) d -> p t d", p=P), y[:]
                             ).then_inc(out_sent, DMA)

            load_x(0, 0)
            load_x(0, 1)
            load_w2(0)
            load_w2(1)
            load_x(0, 2)
            load_x(0, 3)
            load_y(0)
            for b in range(NB):
                for m in range(MT):
                    if b == 0 and m + 2 < MT:
                        load_w2(m + 2)
                    if b + 1 < NB and m < TT:
                        load_x(b + 1, m)
                    if b and m == 3:
                        store(b - 1)
                    if b and m == 5:
                        load_y(b)
            store(NB - 1)
            sp.wait_ge(out_sent, NB * DMA)

        @block.gpsimd
        def _(pool):
            nc.gpsimd.memset(neg_half[:], -0.5).then_inc(half_set, 1)

            def low_w2(m):
                pool.wait_ge(w2_high, m + 1)
                nc.gpsimd.tensor_tensor(w2_l[:, m], w2_raw[m % 2][:], w2_h[:, m].bitcast(F32),
                                        ALU.subtract).then_inc(w2_low, 1)

            def low_g(b, m):
                i = b * MT + m
                pool.wait_ge(g_high, i + 1)
                if i >= 2:
                    pool.wait_ge(out_mm, i - 1)
                nc.gpsimd.tensor_tensor(g_l[m % 2][:], picked[m % 2][:], g_h[m % 2][:].bitcast(F32),
                                        ALU.subtract).then_inc(g_ready, 1)

            def root(b):
                pool.wait_ge(var_ready, b + 1)
                nc.gpsimd.tensor_tensor(rstd[:], var[:], neg_half[:], ALU.pow).then_inc(rstd_ready, 1)

            pool.wait_ge(half_set, 1)
            low_w2(0)
            for b in range(NB):
                for m in range(MT):
                    low_g(b, m)
                    if b == 0 and m + 1 < MT:
                        low_w2(m + 1)
                    if m == 1 and b:
                        root(b - 1)
            root(NB - 1)

        @block.scalar
        def _(act):
            def turn(b, m):
                i = b * MT + m
                act.wait_ge(mask_turned, i + 1)
                if i >= 2:
                    act.wait_ge(z_done, i - 1)
                nc.scalar.activation(mask_t[m % 2][:], ps_t[:], ACT.Copy).then_inc(mask_t_ready, 1)

            def relu(b, m):
                i = b * MT + m
                act.wait_ge(h_done, i + 1)
                if i >= 2:
                    act.wait_ge(picked_ready, i - 1)
                nc.scalar.activation(act_r[m % 2][:], ps_h[:], ACT.Relu).then_inc(relu_ready, 1)

            def high_g(b, m):
                i = b * MT + m
                act.wait_ge(picked_ready, i + 1)
                if i >= 2:
                    act.wait_ge(out_mm, i - 1)
                nc.scalar.activation(g_h[m % 2][:], picked[m % 2][:], ACT.Copy).then_inc(g_high, 1)

            def high_w2(m):
                act.wait_ge(w2_in[m % 2], DMA * (m // 2 + 1))
                nc.scalar.activation(w2_h[:, m], w2_raw[m % 2][:], ACT.Copy).then_inc(w2_high, 1)

            high_w2(0)
            turn(0, 0)
            for b in range(NB):
                for m in range(MT):
                    if b == 0 and m + 1 < MT:
                        high_w2(m + 1)
                    relu(b, m)
                    if b * MT + m + 1 < NB * MT:
                        turn(*divmod(b * MT + m + 1, MT))
                    high_g(b, m)

        @block.vector
        def _(dve):
            def prep(b, s, bank):
                n = number(b, s)
                dve.wait_ge(prep_mm, n + 1)
                if s < TT:
                    dst = [part[b % 2][:, :, s * P:(s + 1) * P] for part in (xt_h, xt_l)]
                    src = bank[:].rearrange("p (k t) -> p k t", k=KT)
                    if s == 0 and b >= 2:
                        dve.wait_ge(h_done, MT * (b - 1))
                    nc.vector.tensor_copy(dst[0], src).then_inc(prep_half, 1)
                    dve.wait_ge(prep_half, n + 1)
                    nc.vector.tensor_tensor(dst[1], src, dst[0].bitcast(F32), ALU.subtract).then_inc(prep_done, 1)
                elif s == U:
                    nc.vector.tensor_copy(u[:], bank[0:80]).then_inc(prep_half, 1)
                    dve.wait_ge(prep_half, n + 1)
                    nc.vector.tensor_tensor(u[32:32 + RANK], bank[32:32 + RANK],
                                            u[32:32 + RANK].bitcast(F32), ALU.subtract).then_inc(prep_done, 1)
                else:
                    c, t = divmod(s - TT - 1, TT)
                    src = bank[:, 0:CH].rearrange("p (n k) -> p n k", k=BLK)
                    nc.vector.tensor_reduce(top[t % 2][:], src, AX.X, ALU.max).then_inc(prep_half, 1)
                    dve.wait_ge(prep_half, n + 1)
                    if b and t == 0:
                        dve.wait_ge(mask_turned, MT * (b - 1) + min(MT, -(-(c + 1) * CH // P)))
                    nc.vector.tensor_tensor(
                        mask[:, t, c * CH:(c + 1) * CH].rearrange("p (n k) -> p n k", k=BLK), src,
                        top[t % 2][:].rearrange("p (n o) -> p n o", o=1).broadcast_to([P, CH // BLK, BLK]),
                        ALU.is_equal).then_inc(prep_done, 1)

            def pick(b, m):
                i = b * MT + m
                dve.wait_ge(z_done, i + 1)
                dve.wait_ge(relu_ready, i + 1)
                if i >= 2:
                    dve.wait_ge(g_ready, i - 1)
                nc.vector.scalar_tensor_tensor(picked[m % 2][:], ps_z[:], 1.0, act_r[m % 2][:], ALU.is_equal,
                                               ALU.mult).then_inc(picked_ready, 1)

            def add(b):
                dve.wait_ge(y_in, DMA * (b + 1))
                dve.wait_ge(out_mm, MT * (b + 1))
                for t in range(TT):
                    nc.vector.tensor_tensor(y[:, t], ps_out[t][:], y[:, t], ALU.add).then_inc(y_ready, 1)

            def statistics(b):
                for t in range(TT):
                    dve.wait_ge(y_ready, TT * b + t + 1)
                    nc.vector.bn_stats(stats[:, t], y[:, t]).then_inc(stat_done, 1)
                for t in range(TT):
                    dve.wait_ge(stat_done, TT * b + t + 1)
                    nc.vector.bn_aggr(mv[:, t], stats[:, t]).then_inc(aggr_done, 1)
                dve.wait_ge(aggr_done, TT * (b + 1))
                nc.vector.tensor_scalar(var[:], mv[:, :, 1], EPS, None, ALU.add).then_inc(var_ready, 1)

            def norm(b):
                dve.wait_ge(rstd_ready, b + 1)
                for t in range(TT):
                    nc.vector.tensor_scalar(y[:, t], y[:, t], mv[:, t, 0:1], rstd[:, t:t + 1],
                                            ALU.subtract, ALU.mult).then_inc(out_ready, 1)

            for s in range(EARLY):
                prep(0, s, (ps_prep, ps_z, ps_h)[s % 3])
            for b in range(NB):
                for m in range(MT):
                    steps = slot_steps(m, b == NB - 1)
                    if steps:
                        prep(b + steps[0][0], steps[0][1], ps_prep)
                    pick(b, m)
                    if len(steps) > 1:
                        prep(b + steps[1][0], steps[1][1], ps_prep)
                    if b and m < 3:
                        (add, statistics, norm)[m](b - 1)
            add(NB - 1)
            statistics(NB - 1)
            norm(NB - 1)

        @block.tensor
        def _(pe):
            def prep(b, s, bank, banks=1):
                n = number(b, s)
                if n >= banks:
                    pe.wait_ge(prep_done, n - banks + 1)
                if s < TT:
                    pe.wait_ge(x_in[s % 2], DMA * (b * TT // 2 + s // 2 + 1))
                    for k in range(KT):
                        last = nc.tensor.transpose(bank[:, k * P:(k + 1) * P], x_sb[s % 2][:, k * P:(k + 1) * P],
                                                   ident[:])
                elif s == U:
                    pe.wait_ge(prep_done, n)
                    for k in range(KT):
                        for i, (c, xx) in enumerate(((c1_h, xt_h), (c1_l, xt_h), (c1_h, xt_l))):
                            last = nc.tensor.matmul(bank[0:80], c[:, k], xx[b % 2][:, k],
                                                    start=(k == 0 and i == 0), stop=(k == KT - 1 and i == 2))
                else:
                    c, t = divmod(s - TT - 1, TT)
                    pe.wait_ge(prep_done, number(b, U) + 1)
                    last = nc.tensor.matmul(bank[:, 0:CH], u[:, t * P:(t + 1) * P], c2_s[:, c * CH:(c + 1) * CH],
                                            start=True, stop=True)
                last.then_inc(prep_mm, 1)

            def turn_mask(b, m):
                i = b * MT + m
                pe.wait_ge(prep_done, number(b, marks(-(-(m + 1) * P // CH) - 1, TT - 1)) + 1)
                if i:
                    pe.wait_ge(mask_t_ready, i)
                for t in range(TT):
                    last = nc.tensor.transpose(ps_t[:, t * P:(t + 1) * P], mask[:, t, m * P:(m + 1) * P], ident16[:])
                last.then_inc(mask_turned, 1)

            def inner_up(b, m, ks):
                i = b * MT + m
                if ks[0] == 0:
                    if i:
                        pe.wait_ge(relu_ready, i)
                    if m == 0:
                        pe.wait_ge(prep_done, number(b, TT - 1) + 1)
                for k in ks:
                    for n, (w, xx) in enumerate(((w1_h, xt_h), (w1_h, xt_l), (w1_l, xt_h))):
                        last = nc.tensor.matmul(ps_h[:], w[:, k, m * P:(m + 1) * P], xx[b % 2][:, k],
                                                start=(k == 0 and n == 0), stop=(k == KT - 1 and n == 2))
                if ks[-1] == KT - 1:
                    last.then_inc(h_done, 1)

            def first_marks(b, m):
                i = b * MT + m
                pe.wait_ge(mask_t_ready, i + 1)
                if i:
                    pe.wait_ge(picked_ready, i)
                nc.tensor.matmul(ps_z[:], first[:], mask_t[m % 2][:], start=True, stop=True).then_inc(z_done, 1)

            def inner_down(b, m, ts):
                i = b * MT + m
                if ts[0] == 0:
                    pe.wait_ge(g_ready, i + 1)
                    if b == 0:
                        pe.wait_ge(w2_low, m + 1)
                for t in ts:
                    if m == 0 and b:
                        pe.wait_ge(y_ready, TT * (b - 1) + t + 1)
                    for n, (g, w) in enumerate(((g_h, w2_h), (g_h, w2_l), (g_l, w2_h))):
                        last = nc.tensor.matmul(ps_out[t][:], g[m % 2][:, t * P:(t + 1) * P], w[:, m],
                                                start=(m == 0 and n == 0), stop=(m == MT - 1 and n == 2))
                if ts[-1] == TT - 1:
                    last.then_inc(out_mm, 1)

            for s in range(EARLY):
                prep(0, s, (ps_prep, ps_z, ps_h)[s % 3], 3)
            pe.wait_ge(prep_done, EARLY)
            turn_mask(0, 0)
            for b in range(NB):
                for m in range(MT):
                    steps = slot_steps(m, b == NB - 1)
                    before = divmod(b * MT + m - 1, MT)
                    inner_up(b, m, (0, 1))
                    if steps:
                        prep(b + steps[0][0], steps[0][1], ps_prep)
                    inner_up(b, m, (2, 3))
                    first_marks(b, m)
                    if b * MT + m:
                        inner_down(*before, (0, 1))
                    if len(steps) > 1:
                        prep(b + steps[1][0], steps[1][1], ps_prep)
                    if b * MT + m:
                        inner_down(*before, (2, 3))
                    if b * MT + m + 1 < NB * MT:
                        turn_mask(*divmod(b * MT + m + 1, MT))
            inner_down(NB - 1, MT - 1, (0, 1, 2, 3))


def _constants(nc, ident, ident16, first):
    with ExitStack() as ctx:
        step = ctx.enter_context(nc.semaphore("const_step"))
        ones = ctx.enter_context(nc.sbuf_tensor("const_f", [P, P], F32))
        block = ctx.enter_context(nc.Block())

        @block.gpsimd
        def _(pool):
            nc.gpsimd.memset(ident[:], 0.0).then_inc(step, 1)
            nc.gpsimd.memset(ones[:], 0.0).then_inc(step, 1)
            pool.wait_ge(step, 2)
            nc.gpsimd.affine_select(out=ident[:], in_=ident[:], compare_op=ALU.not_equal, fill=1.0, base=0,
                                    pattern=[[-1, P]], channel_multiplier=1).then_inc(step, 1)
            nc.gpsimd.affine_select(out=ones[:], in_=ones[:], compare_op=ALU.is_ge, fill=-2.0, base=0,
                                    pattern=[[-1, P]], channel_multiplier=1).then_inc(step, 1)
            pool.wait_ge(step, 4)
            nc.gpsimd.affine_select(out=ones[:].rearrange("p (n k) -> p n k", k=BLK),
                                    in_=ones[:].rearrange("p (n k) -> p n k", k=BLK), compare_op=ALU.is_ge,
                                    fill=0.0, base=0, pattern=[[-BLK, P // BLK], [0, BLK]],
                                    channel_multiplier=1).then_inc(step, 1)
            pool.wait_ge(step, 5)
            nc.gpsimd.affine_select(out=ones[:], in_=ones[:], compare_op=ALU.not_equal, fill=1.0, base=0,
                                    pattern=[[-1, P]], channel_multiplier=1).then_inc(step, 1)
            pool.wait_ge(step, 6)
            nc.gpsimd.tensor_copy(ident16[:], ident[:]).then_inc(step, 1)
            nc.gpsimd.tensor_copy(first[:], ones[:]).then_inc(step, 1)


def build(nc, x, xT, w_qkv, wo, c1, c2, w1, w2, out):
    qs = _scratch(nc, "q_stacks", NB * NKV * Q_UNIT)
    ks = _scratch(nc, "k_stacks", NB * NKV * K_UNIT)
    vs = _scratch(nc, "v_units", NB * NKV * V_UNIT)
    num = _scratch(nc, "weighted_sums", NB * NH * HD * S)
    den = _scratch(nc, "denominators", NB * NH * S)
    rden = _scratch(nc, "reciprocals", NB * NH * S)
    x1 = _scratch(nc, "after_attention", NB * S * D)
    with ExitStack() as ctx:
        sb = lambda name, shape, dt: ctx.enter_context(nc.sbuf_tensor(name, shape, dt))
        ident = sb("ident", [P, P], F32)
        ident16 = sb("ident16", [P, P], BF16)
        first = sb("first", [P, P], BF16)
        c1_h, c1_l = sb("c1_h", [P, KT, 80], F32R), sb("c1_l", [P, KT, 80], F32R)
        c2_s = sb("c2_s", [80, INTER], F32R)
        _constants(nc, ident, ident16, first)
        with ExitStack() as early:
            wo_h = early.enter_context(nc.sbuf_tensor("wo_h", [P, REP, D], F32R, side="right"))
            wo_l = early.enter_context(nc.sbuf_tensor("wo_l", [P, REP, D], F32R, side="right"))
            _project(nc, xT, w_qkv, qs, ks, vs, wo, c1, c2, (wo_h, wo_l, c1_h, c1_l, c2_s))
            w1_h, w1_l = sb("w1_h", [P, KT, INTER], F32R), sb("w1_l", [P, KT, INTER], F32R)
            _attend(nc, x, qs, ks, vs, num, den, rden, x1, wo_h, wo_l, w1, w1_h, w1_l, ident)
        _feed_forward(nc, x1, out, w2, w1_h, w1_l, c1_h, c1_l, c2_s, ident, ident16, first)


def kernel(L0_attn_x, L0_attn_wq, L0_attn_wk, L0_attn_wv, L0_attn_wo, L0_ffn_c1_w, L0_ffn_c2_w, L0_ffn_w1,
           L0_ffn_w2t):
    import numpy as np
    import concourse.bacc as bacc
    from concourse.bass_utils import run_bass_kernel_spmd

    x = np.asarray(L0_attn_x).reshape(NB * S, D)
    wq = np.asarray(L0_attn_wq).reshape(D, NKV, REP, HD).transpose(0, 2, 1, 3).reshape(D, D)
    wo = np.asarray(L0_attn_wo).reshape(NKV, REP, HD, D).transpose(1, 0, 2, 3).reshape(D, D)
    arrays = {
        "x": x, "xT": x.T,
        "w_qkv": np.concatenate([wq, np.asarray(L0_attn_wk), np.asarray(L0_attn_wv)], axis=1),
        "wo": wo, "c1": np.asarray(L0_ffn_c1_w).T, "c2": np.asarray(L0_ffn_c2_w).T,
        "w1": np.asarray(L0_ffn_w1).T, "w2": np.asarray(L0_ffn_w2t),
    }
    arrays = {name: np.ascontiguousarray(a) for name, a in arrays.items()}
    nc = bacc.Bacc("TRN2", target_bir_lowering=False, num_devices=1)
    args = [nc.dram_tensor(name, a.shape, mybir.dt.from_np(a.dtype), kind="ExternalInput").ap()
            for name, a in arrays.items()]
    out = nc.dram_tensor("out", (NB * S, D), F32, kind="ExternalOutput").ap()
    build(nc, *args, out)
    r = run_bass_kernel_spmd(nc, [arrays], core_ids=[0])
    return r.results[0]["out"].reshape(NB, S, D)
```

```python
import concourse.bass as bass
from concourse import mybir
from contextlib import ExitStack

F32 = mybir.dt.float32
F32R = mybir.dt.float32r
BF16 = mybir.dt.bfloat16
ALU = mybir.AluOpType
ACT = mybir.ActivationFunctionType
AX = mybir.AxisListType

P = 128
NB = 4
S = 512
D = 512
NH, NKV = 32, 8
HD = D // NH
REP = NH // NKV
KT = D // P
TT = S // P
KV = NKV * HD
INTER, BLK, RANK = 1792, 32, 16
MT = INTER // P
CH = 448
NC = INTER // CH
EPS = 1e-5
DMA = 16

STACK = 3 * HD
SHIFT = STACK
ROWS = STACK + 2
VW = 2 * HD
VG = NKV // 2
Q_UNIT = 2 * 2 * HD * 2 * S
K_UNIT = STACK * S
V_HALF = P * TT * VG * VW
SUMS = P * S
NU = NB * NKV


def _scratch(nc, name, n):
    return nc.dram_tensor(name, (n,), F32, kind="Internal").ap()


def _projection_memory(nc):
    with ExitStack() as ctx:
        sb = lambda name, shape, dt=F32: ctx.enter_context(nc.sbuf_tensor(name, shape, dt))
        WQ = D + 2 * KV
        return dict(
            w_raw=sb("w_raw", [P, KT, WQ]), w_h=sb("w_h", [P, KT, WQ], F32R), w_l=sb("w_l", [P, KT, WQ], F32R),
            x_raw=[sb(f"x_raw{j}", [P, KT, S]) for j in range(2)],
            x_h=[sb(f"x_h{j}", [P, KT, S], F32R) for j in range(2)],
            x_l=[sb(f"x_l{j}", [P, KT, S], F32R) for j in range(2)],
            wo_raw=sb("wo_raw", [P, REP, D]), c1_raw=sb("c1_raw", [P, KT, 80]), c2_raw=sb("c2_raw", [80, INTER]),
            parts=[sb(f"parts{j}", [P, 2, S], F32R) for j in range(3)],
            v_rows=sb("v_rows", [P, S]), v_new=sb("v_new", [P, TT, NKV, VW]))


def _attend(nc, x, xT, w_qkv, wo, c1, c2, w1, dram, x1, projection, keep):
    qs, ks, vs, sums, rden = dram
    w1_h, w1_l, c1_h, c1_l, c2_s, ident, xt_h, xt_l, u, wo_h, wo_l = keep
    w_raw, w_h, w_l, x_raw, x_h, x_l, wo_raw, c1_raw, c2_raw, parts, v_rows, v_new = projection.values()
    att_h, att_l = xt_h[1], xt_l[1]
    QR = 4
    TASKS = REP + 2
    LAST = NB * TASKS
    FRONT = LAST - TASKS
    FIRST_MAXIMA = FRONT - 8
    with ExitStack() as ctx:
        sb = lambda name, shape, dt=F32: ctx.enter_context(nc.sbuf_tensor(name, shape, dt))
        sem = lambda name: ctx.enter_context(nc.semaphore(name))
        sems = lambda name, n: [sem(f"{name}{j}") for j in range(n)]
        ps = lambda name, shape: ctx.enter_context(nc.psum_tensor(name, shape, F32))
        att, inv = sb("att", [P, REP, S]), sb("inv", [P, REP, S])
        den, inv_den = sb("den", [P, P]), sb("inv_den", [P, P])
        y = sb("y", [P, TT, D])
        x_sb = [sb(f"x_sb{j}", [P, D]) for j in range(2)]
        w1_raw = [sb(f"w1_raw{j}", [P, CH]) for j in range(2)]
        probs = [sb(f"probs{j}", [P, REP, S]) for j in range(2)]
        stage = [sb(f"stage{j}", [P, S]) for j in range(2)]
        q = [sb(f"q{j}", [P, 2, S], F32R) for j in range(QR)]
        k_ = [sb(f"k{j}", [P, S], F32R) for j in range(QR)]
        v = [sb(f"v{j}", [P, TT, VG, VW]) for j in range(2)]
        neg_max = sb("neg_max", [P, TT, 2, 2])
        max_parts = sb("max_parts", [P, TT, 2, 2, 2], F32R)
        shift = [sb(f"shift{j}", [8, S], F32R) for j in range(2)]
        stats, mv = sb("stats", [P, TT, 6]), sb("mv", [P, TT, 2])
        var, rstd, neg_half = sb("var", [P, TT]), sb("rstd", [P, TT]), sb("neg_half", [P, TT])
        ps_max = [ps(f"ps_max{j}", [P, 2, S]) for j in range(2)]
        ps_st = [ps(f"ps_st{j}", [P, S]) for j in range(2)]
        ps_pv = ps("ps_pv", [P, S])
        ps_x = ps("ps_x", [P, S])
        bank = [(*ps_st, ps_pv)[i % 3] if i < FRONT else ps_x for i in range(LAST)]

        w_in, w_high, w_split = sems("w_in", KT), sem("w_high"), sem("w_split")
        xt_in, x_high, x_split = [sems(f"xt_in{j}_", KT) for j in range(2)], sem("x_high"), sem("x_split")
        projected, high_out, evacuated = sem("projected"), sem("high_out"), sem("evacuated")
        v_copied, v_turned = sem("v_copied"), sem("v_turned")
        ones_set, part_out, v_out = sem("ones_set"), sems("part_out", 3), sem("v_out")
        pre_in, pre_zero, pre = sem("pre_in"), sem("pre_zero"), sem("pre")
        unit_in, v_in, shift_in = sems("unit_in", QR), sems("v_in", 2), sems("shift_in", QR)
        max_mm, max_red = sem("max_mm"), sem("max_red")
        max_high, max_split, max_turned, shift_ready = (sem("max_high"), sem("max_split"),
                                                        sem("max_turned"), sem("shift_ready"))
        st_mm, exp_done, pv_done, stage_ready = sem("st_mm"), sem("exp_done"), sem("pv_done"), sem("stage_ready")
        stage_out, sums_in = sems("stage_out", 2), sem("sums_in")
        rden_out, inv_in = sem("rden_out"), sem("inv_in")
        inverted, att_scaled, att_high, att_split = (sem("inverted"), sem("att_scaled"), sem("att_high"),
                                                     sem("att_split"))
        wo_done, x_in, y_ready = sem("wo_done"), sems("xr_in", 2), sem("y_ready")
        stat_done, aggr_done, var_ready, rstd_ready = (sem("stat_done"), sem("aggr_done"),
                                                       sem("var_ready"), sem("rstd_ready"))
        powers_set, x1_ready, x1_out = sem("powers_set"), sem("x1_ready"), sem("x1_out")
        w1_in, w1_high, w1_low = sems("w1_in", 2), sem("w1_high"), sem("w1_low")
        f_in, turned_mm, turned_high, turned = sems("f_in", 2), sem("turned_mm"), sem("turned_high"), sem("turned")
        LOADS = 6
        SHIFT_TASK = 3
        LATE_AT = ((0, -1), (0, 2), (1, 0), (1, 2), (2, 0), (2, 2))
        WO_AT = ((5, 0), (5, 2), (6, 0), (6, 2))
        HIGH_AT = ((3, 2), (3, 3), (4, 0), (4, 1))
        block = ctx.enter_context(nc.Block())

        def parts_out(m, j):
            return sum(2 if i % (REP + 1) == REP else 1 for i in range(m) if i % 3 == j)

        def maxima_at(b, s):
            at = 2 * (TASKS * b + s - FIRST_MAXIMA)
            end = 16 if TASKS * b + s == FRONT - 1 else at + 2
            return [divmod(i, 8) for i in range(at, end) if i >= 0]

        def in_sbuf(b, s):
            return TASKS * b + (s + 1 if s > 1 or b == NB - 1 else 2 - s)

        def projections_done(eng):
            eng.wait_ge(evacuated, LAST)
            for j in range(3):
                eng.wait_ge(part_out[j], DMA * parts_out(NB * (REP + 1), j))
            eng.wait_ge(v_out, 2 * DMA * NB)
            eng.wait_ge(pre, 6)

        @block.sync
        def _(sp):
            def load_x(b, k):
                if b >= 2:
                    sp.wait_ge(x_split, KT * (b - 1))
                sp.dma_start(x_raw[b % 2][:, k], xT[b, k * P:(k + 1) * P]).then_inc(xt_in[b % 2][k], DMA)

            def store_projection(b, s):
                sp.wait_ge(evacuated, in_sbuf(b, s))
                if s == 0:
                    for f in range(2):
                        at = (2 * b + f) * V_HALF
                        sp.dma_start(vs[at:at + V_HALF].rearrange("(p k g c) -> p k g c", p=P, k=TT, g=VG),
                                     v_new[:, :, f * VG:(f + 1) * VG]).then_inc(v_out, DMA)
                    return
                s -= 1
                j = ((REP + 1) * b + s) % 3
                src = parts[j][:].bitcast(F32)
                if s < REP:
                    dst = qs[b * NKV * Q_UNIT:(b + 1) * NKV * Q_UNIT].rearrange(
                        "(p a s j t) -> a j p s t", p=P, a=2, s=2, j=2)[s % 2, s // 2]
                    sp.dma_start(dst, src).then_inc(part_out[j], DMA)
                else:
                    dst = ks[b * NKV * K_UNIT:(b + 1) * NKV * K_UNIT].rearrange("(p s t) -> p s t", p=P, s=3)
                    sp.dma_start(dst[:, 0], src[:, 0]).then_inc(part_out[j], DMA)
                    sp.dma_start(dst[:, 1:3], src).then_inc(part_out[j], DMA)

            def load_unit(n):
                j, b = n % QR, n // NKV
                if n >= QR:
                    sp.wait_ge(pv_done, TT * (n - QR + 1))
                elif n == 0:
                    sp.wait_ge(ones_set, 2 * QR + 1)
                if n % NKV == 0:
                    for i in range(3):
                        sp.wait_ge(part_out[i], DMA * parts_out((b + 1) * (REP + 1), i))
                q_src = qs[n * Q_UNIT:(n + 1) * Q_UNIT].rearrange("(d a s t) -> a s d t", d=HD, a=2, s=2)
                k_src = ks[n * K_UNIT:(n + 1) * K_UNIT].rearrange("(d s t) -> s d t", d=HD, s=3)
                for a in range(2):
                    for dst, src in ((q[j][64 * a:64 * a + 2 * HD], q_src[a]),
                                     (q[j][64 * a + 2 * HD:64 * a + STACK], q_src[a, 0]),
                                     (k_[j][64 * a:64 * a + STACK], k_src)):
                        sp.dma_start(dst.bitcast(F32), src).then_inc(unit_in[j], DMA)

            def load_v(f):
                if f >= 2:
                    sp.wait_ge(pv_done, TT * VG * (f - 1))
                sp.wait_ge(v_out, 2 * DMA * (f // 2 + 1))
                sp.dma_start(v[f % 2][:].rearrange("p k g c -> p (k g c)"),
                             vs[f * V_HALF:(f + 1) * V_HALF].rearrange("(p c) -> p c", p=P)).then_inc(v_in[f % 2], DMA)

            def send_shift(n):
                sp.wait_ge(shift_ready, n + 1)
                for a in range(2):
                    sp.dma_start(q[n % QR][64 * a + SHIFT:64 * a + SHIFT + 2].bitcast(F32),
                                 shift[n % 2][4 * a:4 * a + 4].bitcast(F32)
                                 ).then_inc(shift_in[n % QR], DMA)

            def store_unit(n):
                sp.wait_ge(stage_ready, n + 1)
                sp.dma_start(sums[n * SUMS:(n + 1) * SUMS].rearrange("(p t) -> p t", p=P), stage[n % 2][:]
                             ).then_inc(stage_out[n % 2], DMA)

            def load_sums(n):
                b, g = n // NKV, n % NKV
                if g == 0 and b:
                    sp.wait_ge(att_split, REP * b)
                sp.wait_ge(stage_out[n % 2], DMA * (n // 2 + 1))
                src = sums[n * SUMS:(n + 1) * SUMS].rearrange("(r h d t) -> h d r t", r=REP, h=2, d=HD)
                sp.dma_start(att[HD * g:HD * (g + 1)], src[0]).then_inc(sums_in, DMA)
                sp.dma_start(den[HD * g:HD * (g + 1)], src[1, 0].rearrange("r (n t) -> r n t", t=P)
                             ).then_inc(sums_in, DMA)

            def spread_reciprocals(b):
                at = b * NH * S
                sp.wait_ge(inverted, b + 1)
                sp.dma_start(rden[at:at + NH * S].rearrange("(p t) -> p t", p=P), inv_den[:]).then_inc(rden_out, DMA)
                sp.wait_ge(rden_out, DMA * (b + 1))
                sp.dma_start(inv[:].rearrange("p r t -> p (r t)"),
                             rden[at:at + NH * S].rearrange("(g o t) -> g o t", g=NKV, o=1).broadcast_to(
                                 [NKV, HD, REP * S])).then_inc(inv_in, DMA)

            def load_residual(b, t):
                i = b * TT + t
                if i >= 2:
                    sp.wait_ge(y_ready, i - 1)
                sp.dma_start(x_sb[i % 2][:], x[i * P * D:(i + 1) * P * D].rearrange("(p d) -> p d", p=P)
                             ).then_inc(x_in[i % 2], DMA)

            def store_x1(b):
                sp.wait_ge(x1_ready, TT * (b + 1))
                sp.dma_start(x1[b * S * D:(b + 1) * S * D].rearrange("(t p d) -> p t d", t=TT, p=P),
                             y[:]).then_inc(x1_out, DMA)

            def load_f(t):
                if t < 2:
                    sp.wait_ge(y_ready, TT * (NB - 1))
                    sp.wait_ge(x1_out, DMA)
                else:
                    sp.wait_ge(turned_mm, t - 1)
                sp.dma_start(x_sb[t % 2][:], x1[t * P * D:(t + 1) * P * D].rearrange("(p d) -> p d", p=P)
                             ).then_inc(f_in[t % 2], DMA)

            for k in range(KT):
                load_x(0, k)
                sp.dma_start(w_raw[:, k], w_qkv[k * P:(k + 1) * P]).then_inc(w_in[k], DMA)
            for k in range(KT):
                load_x(1, k)
            for b in range(NB):
                if b + 2 < NB:
                    for k in range(KT):
                        load_x(b + 2, k)
                for s in range(TASKS if b < NB - 1 else 0):
                    store_projection(b, s)
                    if b == NB - 2 and s == SHIFT_TASK:
                        send_shift(0)
                    if b == 1 and s in (1, 3):
                        load_unit(1 + (1, 3).index(s))
                if b == 0:
                    load_unit(0)
                if b == 1:
                    load_v(0)
                    load_v(1)
            for n in range(NU):
                b, g = n // NKV, n % NKV
                if n == NU - 1:
                    load_f(0)
                    load_f(1)
                if n:
                    store_unit(n - 1)
                if n + 3 < NU:
                    load_unit(n + 3)
                if g % VG == 1 and 1 < n // VG + 1 < 2 * NB:
                    load_v(n // VG + 1)
                if n + 1 < NU:
                    send_shift(n + 1)
                for t in range(TT):
                    if b and WO_AT[t][0] == g + 1:
                        load_residual(b - 1, t)
                if n == NU - 1:
                    load_f(2)
                    load_f(3)
                for t in range(TASKS):
                    if not b and LATE_AT[t][0] == g:
                        store_projection(NB - 1, t)
                if n == 4:
                    projections_done(sp)
                for i in {2: (), 3: (), 4: (n - 4, n - 3, n - 2)}.get(g, (n - 2,)):
                    if i >= 0:
                        load_sums(i)
                if b and g == 2:
                    spread_reciprocals(b - 1)
                if b > 1 and g == 0:
                    store_x1(b - 2)
            store_unit(NU - 1)
            load_sums(NU - 2)
            load_sums(NU - 1)
            spread_reciprocals(NB - 1)
            store_x1(NB - 2)
            sp.wait_ge(x1_out, (NB - 1) * DMA)

        @block.gpsimd
        def _(pool):
            nc.gpsimd.memset(neg_half[:], -0.5).then_inc(powers_set, 1)
            nc.gpsimd.memset(c1_raw[:], 0.0).then_inc(pre_zero, 1)
            nc.gpsimd.memset(c2_raw[:], 0.0).then_inc(pre_zero, 1)
            pool.dma_start(wo_raw[:], wo.rearrange("(r p) n -> p r n", p=P)).then_inc(pre_in, DMA)
            pool.wait_ge(pre_zero, 2)
            for n in range(3):
                pool.dma_start(c1_raw[:, :, 32 * n:32 * n + RANK],
                               c1.rearrange("(k p) n -> p k n", p=P)).then_inc(pre_in, DMA)
                pool.dma_start(c2_raw[32 * n:32 * n + RANK, :], c2).then_inc(pre_in, DMA)
            pool.wait_ge(pre_in, 7 * DMA)
            nc.gpsimd.tensor_copy(wo_h[:], wo_raw[:]).then_inc(pre, 1)
            nc.gpsimd.tensor_copy(c1_h[:], c1_raw[:]).then_inc(pre, 1)
            nc.gpsimd.tensor_copy(c2_s[:], c2_raw[:]).then_inc(pre, 1)
            pool.wait_ge(pre, 3)
            nc.gpsimd.tensor_tensor(wo_l[:], wo_raw[:], wo_h[:].bitcast(F32), ALU.subtract).then_inc(pre, 1)
            nc.gpsimd.tensor_tensor(c1_l[:], c1_raw[:], c1_h[:].bitcast(F32), ALU.subtract).then_inc(pre, 1)
            pool.wait_ge(pre, 5)
            nc.gpsimd.tensor_tensor(c2_s[64:80], c2_raw[64:80], c2_s[64:80].bitcast(F32),
                                    ALU.subtract).then_inc(pre, 1)

            w1_v = w1.rearrange("(k p) n -> p k n", p=P)
            projections_done(pool)

            def load_w1(i):
                if i >= 2:
                    pool.wait_ge(w1_low, i - 1)
                pool.dma_start(w1_raw[i % 2][:], w1_v[:, i // NC, (i % NC) * CH:(i % NC + 1) * CH]
                               ).then_inc(w1_in[i % 2], DMA)
            load_w1(0)
            for i in range(KT * NC):
                if i + 1 < KT * NC:
                    load_w1(i + 1)
                k, c = i // NC, i % NC
                pool.wait_ge(w1_in[i % 2], DMA * (i // 2 + 1))
                nc.gpsimd.tensor_copy(w1_h[:, k, c * CH:(c + 1) * CH], w1_raw[i % 2][:]).then_inc(w1_high, 1)
                pool.wait_ge(w1_high, i + 1)
                nc.gpsimd.tensor_tensor(w1_l[:, k, c * CH:(c + 1) * CH], w1_raw[i % 2][:],
                                        w1_h[:, k, c * CH:(c + 1) * CH].bitcast(F32),
                                        ALU.subtract).then_inc(w1_low, 1)
            pool.wait_ge(powers_set, 1)
            for b in range(NB - 1):
                pool.wait_ge(inv_in, DMA * (b + 1))
                for r in range(REP):
                    nc.gpsimd.tensor_tensor(att[:, r], att[:, r], inv[:, r], ALU.mult).then_inc(att_scaled, 1)
                for r in range(REP):
                    pool.wait_ge(att_high, REP * b + r + 1)
                    nc.gpsimd.tensor_tensor(att_l[:, r], att[:, r], att_h[:, r].bitcast(F32), ALU.subtract
                                            ).then_inc(att_split, 1)
                pool.wait_ge(var_ready, b + 1)
                nc.gpsimd.tensor_tensor(rstd[:], var[:], neg_half[:], ALU.pow).then_inc(rstd_ready, 1)

        @block.scalar
        def _(act):
            def high_x(b, k):
                act.wait_ge(xt_in[b % 2][k], DMA * (b // 2 + 1))
                if b >= 2 and k == 0:
                    act.wait_ge(projected, TASKS * (b - 1))
                nc.scalar.activation(x_h[b % 2][:, k], x_raw[b % 2][:, k], ACT.Copy).then_inc(x_high, 1)

            def copy_v(b):
                act.wait_ge(projected, TASKS * b + 1)
                if b:
                    act.wait_ge(v_turned, b)
                nc.scalar.activation(v_rows[:], bank[TASKS * b][:], ACT.Copy).then_inc(v_copied, 1)

            def high_projection(b, s):
                i = TASKS * b + s
                m = (REP + 1) * b + s - 1
                act.wait_ge(projected, i + 1)
                if m >= 3:
                    act.wait_ge(part_out[m % 3], DMA * parts_out(m, m % 3))
                nc.scalar.activation(parts[m % 3][:, 0], bank[i][:], ACT.Copy).then_inc(high_out, 1)

            def turn_shift(n):
                act.wait_ge(max_turned, n + 1)
                if n >= 2:
                    act.wait_ge(shift_in[(n - 2) % QR], 2 * DMA * ((n - 2) // QR + 1))
                nc.scalar.activation(shift[n % 2][:], ps_x[0:8], ACT.Copy).then_inc(shift_ready, 1)

            def take_sums(n):
                act.wait_ge(pv_done, TT * (n + 1))
                if n >= 2:
                    act.wait_ge(stage_out[n % 2], DMA * (n // 2))
                nc.scalar.activation(stage[n % 2][:], ps_pv[:], ACT.Copy).then_inc(stage_ready, 1)

            def high_att(b, r):
                act.wait_ge(att_scaled, REP * b + r + 1)
                if b and r == 0:
                    act.wait_ge(wo_done, TT * b)
                nc.scalar.activation(att_h[:, r], att[:, r], ACT.Copy).then_inc(att_high, 1)

            for k in range(KT):
                high_x(0, k)
                act.wait_ge(w_in[k], DMA)
                nc.scalar.activation(w_h[:, k], w_raw[:, k], ACT.Copy).then_inc(w_high, 1)
            for k in range(KT):
                high_x(1, k)
            for b in range(NB - 1):
                copy_v(b)
                for s in range(1, TASKS):
                    high_projection(b, s)
                    if b == NB - 2 and s == SHIFT_TASK:
                        turn_shift(0)
                if b + 2 < NB:
                    for k in range(KT):
                        high_x(b + 2, k)
            copy_v(NB - 1)
            for n in range(NU):
                b, g = n // NKV, n % NKV
                for kt in range(TT):
                    for r in range(REP):
                        i = (n * TT + kt) * REP + r
                        if r == 2 and not b and (g, kt) in LATE_AT[1:]:
                            high_projection(NB - 1, LATE_AT.index((g, kt)))
                        act.wait_ge(st_mm, i + 1)
                        if r == 0 and n * TT + kt >= 2:
                            act.wait_ge(pv_done, n * TT + kt - 1)
                        nc.scalar.activation(probs[kt % 2][:, r], ps_st[r % 2][:], ACT.Exp,
                                             scale=float(HD) ** -0.5).then_inc(exp_done, 1)
                        if b and r == 2 and (g, kt) in HIGH_AT:
                            high_att(b - 1, HIGH_AT.index((g, kt)))
                    if kt == 0:
                        if n:
                            take_sums(n - 1)
                    if kt == 1 and n + 1 < NU:
                        turn_shift(n + 1)
            take_sums(NU - 1)
            for r in range(REP):
                high_att(NB - 1, r)

        @block.vector
        def _(dve):
            def low_x(b, k):
                dve.wait_ge(x_high, KT * b + k + 1)
                nc.vector.tensor_tensor(x_l[b % 2][:, k], x_raw[b % 2][:, k], x_h[b % 2][:, k].bitcast(F32),
                                        ALU.subtract).then_inc(x_split, 1)

            def row_max(n, i):
                dve.wait_ge(max_mm, 8 * n + i + 1)
                if n and i == 0:
                    dve.wait_ge(max_split, n)
                nc.vector.tensor_reduce(neg_max[:, i // 2, :, i % 2], ps_max[i % 2][:], AX.X, ALU.max,
                                        negate=True).then_inc(max_red, 1)

            def split_max(n):
                dve.wait_ge(max_red, 8 * (n + 1))
                if n:
                    dve.wait_ge(max_turned, n)
                nc.vector.tensor_copy(max_parts[:, :, :, 0], neg_max[:]).then_inc(max_high, 1)
                dve.wait_ge(max_high, n + 1)
                nc.vector.tensor_tensor(max_parts[:, :, :, 1], neg_max[:], max_parts[:, :, :, 0].bitcast(F32),
                                        ALU.subtract).then_inc(max_split, 1)

            def invert(b):
                dve.wait_ge(sums_in, 2 * DMA * NKV * (b + 1))
                if b:
                    dve.wait_ge(rden_out, DMA * b)
                nc.vector.reciprocal(inv_den[:], den[:]).then_inc(inverted, 1)

            def add_tile(b, t):
                i = b * TT + t
                dve.wait_ge(wo_done, i + 1)
                dve.wait_ge(x_in[i % 2], DMA * (i // 2 + 1))
                if b and t == 0:
                    dve.wait_ge(x1_out, DMA * b)
                nc.vector.tensor_tensor(y[:, t], ps_x[:], x_sb[i % 2][:], ALU.add).then_inc(y_ready, 1)
                dve.wait_ge(y_ready, i + 1)
                nc.vector.bn_stats(stats[:, t], y[:, t]).then_inc(stat_done, 1)
                dve.wait_ge(stat_done, i + 1)
                nc.vector.bn_aggr(mv[:, t], stats[:, t]).then_inc(aggr_done, 1)

            def variance(b):
                dve.wait_ge(aggr_done, TT * (b + 1))
                nc.vector.tensor_scalar(var[:], mv[:, :, 1], EPS, None, ALU.add).then_inc(var_ready, 1)

            def norm(b, t):
                dve.wait_ge(rstd_ready, b + 1)
                nc.vector.tensor_scalar(y[:, t], y[:, t], mv[:, t, 0:1], rstd[:, t:t + 1],
                                        ALU.subtract, ALU.mult).then_inc(x1_ready, 1)

            def evacuate(b, s):
                i = TASKS * b + s
                if s:
                    m = (REP + 1) * b + s - 1
                    dve.wait_ge(high_out, m + 1)
                    nc.vector.tensor_tensor(parts[m % 3][:, 1], bank[i][:], parts[m % 3][:, 0].bitcast(F32),
                                            ALU.subtract).then_inc(evacuated, 1)
                else:
                    dve.wait_ge(v_turned, b + 1)
                    if b:
                        dve.wait_ge(v_out, 2 * DMA * b)
                    nc.vector.tensor_copy(v_new[:, :, :, 0:HD],
                                          ps_x[:].rearrange("p (k g d) -> p k g d", k=TT, g=NKV)
                                          ).then_inc(evacuated, 1)

            for j in range(QR):
                for a in range(2):
                    nc.vector.memset(k_[j][64 * a + 32:64 * a + 64].bitcast(F32), 1.0).then_inc(ones_set, 1)
            nc.vector.memset(v_new[:, :, :, HD:VW], 1.0).then_inc(ones_set, 1)
            for k in range(KT):
                low_x(0, k)
                dve.wait_ge(w_high, k + 1)
                nc.vector.tensor_tensor(w_l[:, k], w_raw[:, k], w_h[:, k].bitcast(F32),
                                        ALU.subtract).then_inc(w_split, 1)
            for k in range(KT):
                low_x(1, k)
            for b in range(NB - 1):
                for s in range(TASKS):
                    if s < 2:
                        evacuate(b, 1 - s)
                    else:
                        evacuate(b, s)
                    for n, i in maxima_at(b, s):
                        row_max(n, i)
                        if (n, i) == (0, 7):
                            split_max(0)
                if b + 2 < NB:
                    for k in range(KT):
                        low_x(b + 2, k)
            split_max(1)
            for n in range(NU):
                b, g = n // NKV, n % NKV
                if n + 2 < NU:
                    for i in range(8):
                        row_max(n + 2, i)
                        if not b and i % 2 == 0 and (g, i // 2) in LATE_AT[1:]:
                            evacuate(NB - 1, LATE_AT.index((g, i // 2)))
                        if not b and i % 2 == 0 and (g, i // 2 - 1) == LATE_AT[0]:
                            evacuate(NB - 1, 0)
                        if b and (g, i) == (2, 0):
                            invert(b - 1)
                        if b and i % 2 == 0 and (g, i // 2) in WO_AT:
                            add_tile(b - 1, WO_AT.index((g, i // 2)))
                        if b and g == 7 and i >= 4:
                            norm(b - 1, i - 4)
                    split_max(n + 2)
                if b and g == 6:
                    if n + 2 >= NU:
                        for t in range(2, TT):
                            add_tile(b - 1, t)
                    variance(b - 1)
                if n == NU - 1:
                    for t in range(TT):
                        norm(b - 1, t)
            for t in range(TT):
                dst = [part[0][:, :, t * P:(t + 1) * P] for part in (xt_h, xt_l)]
                src = ps_max[t % 2][:, 0].rearrange("p (k t) -> p k t", k=KT)
                dve.wait_ge(turned_mm, t + 1)
                nc.vector.tensor_copy(dst[0], src).then_inc(turned_high, 1)
                dve.wait_ge(turned_high, t + 1)
                nc.vector.tensor_tensor(dst[1], src, dst[0].bitcast(F32), ALU.subtract).then_inc(turned, 1)
            invert(NB - 1)
            dve.wait_ge(turned_mm, TT + 1)
            nc.vector.tensor_copy(u[:], ps_max[0][0:80, 0]).then_inc(turned_high, 1)
            dve.wait_ge(turned_high, TT + 1)
            nc.vector.tensor_tensor(u[32:32 + RANK], ps_max[0][32:32 + RANK, 0],
                                    u[32:32 + RANK].bitcast(F32), ALU.subtract).then_inc(turned, 1)
            dve.wait_ge(inv_in, DMA * NB)
            for r in range(REP):
                nc.vector.tensor_tensor(att[:, r], att[:, r], inv[:, r], ALU.mult).then_inc(att_scaled, 1)
            for r in range(REP):
                dve.wait_ge(att_high, REP * (NB - 1) + r + 1)
                nc.vector.tensor_tensor(att_l[:, r], att[:, r], att_h[:, r].bitcast(F32), ALU.subtract
                                        ).then_inc(att_split, 1)

        @block.tensor
        def _(pe):
            def project(b, s):
                i = TASKS * b + s
                xs, ws = (x_h, x_h, x_l), (w_h, w_l, w_h)
                if i >= 3:
                    pe.wait_ge(evacuated, i - 2 if i < FRONT else i)
                at = (s - 1) * P if s else D + KV
                for k in range(KT):
                    if s == 0:
                        pe.wait_ge(x_split, KT * b + k + 1)
                        if b == 0:
                            pe.wait_ge(w_split, k + 1)
                    for n in range(3):
                        last = nc.tensor.matmul(bank[i][:], ws[n][:, k, at:at + P], xs[n][b % 2][:, k],
                                                start=(k == 0 and n == 0), stop=(k == KT - 1 and n == 2))
                last.then_inc(projected, 1)

            def turn_v(b):
                pe.wait_ge(v_copied, b + 1)
                if 0 < b < NB - 1:
                    pe.wait_ge(evacuated, in_sbuf(b - 1, 0))
                for t in range(TT):
                    last = nc.tensor.transpose(ps_x[:, t * P:(t + 1) * P], v_rows[:, t * P:(t + 1) * P], ident[:])
                last.then_inc(v_turned, 1)

            def scores(n, i, a):
                if n >= NU:
                    return
                if a == 0:
                    if i == 0:
                        pe.wait_ge(unit_in[n % QR], LOADS * DMA * (n // QR + 1))
                    if 8 * n + i >= 2:
                        pe.wait_ge(max_red, 8 * n + i - 1)
                t, j = i // 2, i % 2
                mm = nc.tensor.matmul(ps_max[i % 2][:, a], q[n % QR][64 * a:64 * a + STACK, j, t * P:(t + 1) * P],
                                      k_[n % QR][64 * a:64 * a + STACK, :], start=True, stop=True)
                if a == 1:
                    mm.then_inc(max_mm, 1)

            def turn_max(n):
                pe.wait_ge(max_split, n + 1)
                b, g = (n - 1) // NKV, (n - 1) % NKV
                tiles = TT * (b - 1) + sum(at <= (g, 1) for at in WO_AT)
                if tiles > 0:
                    pe.wait_ge(y_ready, tiles)
                elif n == 0:
                    pe.wait_ge(evacuated, in_sbuf(NB - 2, 0))
                else:
                    pe.wait_ge(evacuated, FRONT + sum(at <= (n - 1, 1) for at in LATE_AT))
                if n >= 1:
                    pe.wait_ge(shift_ready, n)
                for t in range(TT):
                    last = nc.tensor.transpose(ps_x[0:8, t * P:(t + 1) * P],
                                               max_parts[:, t].rearrange("p a h j -> p (a h j)").bitcast(F32), ident[:])
                last.then_inc(max_turned, 1)

            def scores_t(n, kt, r):
                i = (n * TT + kt) * REP + r
                if kt == 0 and r == 0:
                    pe.wait_ge(shift_in[n % QR], 2 * DMA * (n // QR + 1))
                if i >= 2:
                    pe.wait_ge(exp_done, i - 1)
                else:
                    pe.wait_ge(evacuated, FRONT - 2 + i)
                a, j = r % 2, r // 2
                nc.tensor.matmul(ps_st[r % 2][:], k_[n % QR][64 * a:64 * a + ROWS, kt * P:(kt + 1) * P],
                                 q[n % QR][64 * a:64 * a + ROWS, j, :], start=True, stop=True).then_inc(st_mm, 1)

            def weigh(n, kt):
                f, g = n // VG, n % VG
                pe.wait_ge(exp_done, (n * TT + kt + 1) * REP)
                if kt == 0 and n:
                    pe.wait_ge(stage_ready, n)
                elif kt == 0:
                    pe.wait_ge(evacuated, FRONT)
                if kt == 0 and g == 0:
                    pe.wait_ge(v_in[f % 2], DMA * (f // 2 + 1))
                for r in range(REP):
                    last = nc.tensor.matmul(ps_pv[32 * r:32 * r + VW], v[f % 2][:, kt, g], probs[kt % 2][:, r],
                                            start=(kt == 0), stop=(kt == TT - 1))
                last.then_inc(pv_done, 1)

            def project_out(b, t, turns):
                i = b * TT + t
                if t == 0:
                    pe.wait_ge(att_split, REP * (b + 1))
                    if b == 0:
                        pe.wait_ge(pre, 6)
                if i:
                    pe.wait_ge(y_ready, i)
                pe.wait_ge(shift_ready, turns)
                for r in range(REP):
                    for n, (a, w) in enumerate(((att_h, wo_h), (att_h, wo_l), (att_l, wo_h))):
                        last = nc.tensor.matmul(ps_x[:], a[:, r, t * P:(t + 1) * P], w[:, r],
                                                start=(r == 0 and n == 0), stop=(r == REP - 1 and n == 2))
                last.then_inc(wo_done, 1)

            def turn_x(t):
                pe.wait_ge(f_in[t % 2], DMA * (t // 2 + 1))
                if t >= 2:
                    pe.wait_ge(turned, t - 1)
                elif t == 0:
                    pe.wait_ge(max_red, 8 * NU)
                for k in range(KT):
                    last = nc.tensor.transpose(ps_max[t % 2][:, 0, k * P:(k + 1) * P], x_sb[t % 2][:, k * P:(k + 1) * P],
                                               ident[:])
                last.then_inc(turned_mm, 1)

            for b in range(NB - 1):
                for s in range(TASKS):
                    project(b, s)
                    if s == 1:
                        turn_v(b)
                    for n, i in maxima_at(b, s):
                        scores(n, i, 0)
                        scores(n, i, 1)
                        if (n, i) == (1, 0):
                            turn_max(0)
            pe.wait_ge(shift_ready, 1)
            project(NB - 1, 0)
            for n in range(NU):
                b, g = n // NKV, n % NKV
                for kt in range(TT):
                    scores_t(n, kt, 0)
                    if n == 0 and kt == 0:
                        scores(2, 0, 0)
                    scores(n + 2, 2 * kt, 1)
                    scores_t(n, kt, 1)
                    if kt or n:
                        weigh(*divmod(n * TT + kt - 1, TT))
                    if not b and (g, kt - 1) == LATE_AT[0]:
                        turn_v(NB - 1)
                    if not b and (g, kt) in LATE_AT:
                        pe.wait_ge(shift_ready, n + 1 + (kt > 1))
                        project(NB - 1, LATE_AT.index((g, kt)))
                    if b and (g, kt) in WO_AT:
                        project_out(b - 1, WO_AT.index((g, kt)), min(NU, n + 1 + (kt > 1)))
                    if n == NU - 1 and kt:
                        turn_x(kt - 1)
                    scores_t(n, kt, 2)
                    scores(n + 2, 2 * kt + 1, 0)
                    scores_t(n, kt, 3)
                    scores(n + 2, 2 * kt + 1, 1)
                    scores(*divmod(8 * (n + 2) + 2 * kt + 2, 8), 0)
                    if kt == 1 and n + 1 < NU:
                        turn_max(n + 1)
            weigh(NU - 1, TT - 1)
            turn_x(TT - 1)
            pe.wait_ge(turned, TT)
            for k in range(KT):
                for i, (c, xx) in enumerate(((c1_h, xt_h), (c1_l, xt_h), (c1_h, xt_l))):
                    last = nc.tensor.matmul(ps_max[0][0:80, 0], c[:, k], xx[0][:, k],
                                            start=(k == 0 and i == 0), stop=(k == KT - 1 and i == 2))
            last.then_inc(turned_mm, 1)


def _feed_forward(nc, x, x1, out, w2, keep, ident16, first):
    w1_h, w1_l, c1_h, c1_l, c2_s, ident, xt_h, xt_l, u, wo_h, wo_l = keep
    att_h, att_l = xt_h[1], xt_l[1]
    U = TT
    W2_OWN = MT - REP
    marks = lambda c, t: TT + 1 + c * TT + t
    with ExitStack() as ctx:
        sb = lambda name, shape, dt=F32: ctx.enter_context(nc.sbuf_tensor(name, shape, dt))
        sem = lambda name: ctx.enter_context(nc.semaphore(name))
        ps = lambda name, shape, dt=F32: ctx.enter_context(nc.psum_tensor(name, shape, dt))
        w2_h = sb("w2_h", [P, W2_OWN, D], F32R)
        w2_l = sb("w2_l", [P, W2_OWN, D], F32R)
        w2_raw = [sb(f"w2_raw{j}", [P, D]) for j in range(2)]
        x_sb = [sb(f"xf_sb{j}", [P, D]) for j in range(2)]
        top = [sb(f"top{j}", [P, CH // BLK]) for j in range(2)]
        mask = sb("mask", [P, TT, INTER], BF16)
        mask_t = [sb(f"mask_t{j}", [P, S], BF16) for j in range(2)]
        act_r = [sb(f"relu{j}", [P, S]) for j in range(2)]
        picked = [sb(f"picked{j}", [P, S]) for j in range(2)]
        g_h = [sb(f"g_h{j}", [P, S], F32R) for j in range(2)]
        g_l = [sb(f"g_l{j}", [P, S], F32R) for j in range(2)]
        y = sb("yf", [P, TT, D])
        stats = sb("statsf", [P, TT, 6])
        mv = sb("mvf", [P, TT, 2])
        var = sb("varf", [P, TT])
        rstd = sb("rstdf", [P, TT])
        neg_half = sb("neg_halff", [P, TT])
        ps_out = [ps(f"ps_out{t}", [P, D]) for t in range(TT)]
        ps_h, ps_z, ps_prep = ps("ps_h", [P, S]), ps("ps_z", [P, S]), ps("ps_prep", [P, S])
        ps_t = ps("ps_t", [P, S], BF16)

        x_in = [sem(f"xf_in{j}") for j in range(2)]
        prep_mm, prep_half, prep_done = sem("prep_mm"), sem("prep_half"), sem("prep_done")
        mask_turned, mask_t_ready = sem("mask_turned"), sem("mask_t_ready")
        h_done, relu_ready, z_done, picked_ready = (sem("h_done"), sem("relu_ready"), sem("z_done"),
                                                    sem("picked_ready"))
        g_high, g_ready, out_mm = sem("g_high"), sem("g_ready"), sem("out_mm")
        w2_in, w2_high, w2_low = [sem("w2_in0"), sem("w2_in1")], sem("w2_high"), sem("w2_low")
        y_in, y_ready, stat_done, aggr_done = sem("yf_in"), sem("yf_ready"), sem("statf_done"), sem("aggrf_done")
        half_set, var_ready, rstd_ready = sem("halff_set"), sem("varf_ready"), sem("rstdf_ready")
        x1_out = sem("x1f_out")
        out_ready, out_sent = sem("out_ready"), sem("out_sent")
        block = ctx.enter_context(nc.Block())

        def slot_steps(b, m):
            own = {0: ((1, 0), (1, 1)), 1: ((1, 2), (1, 3)), 2: ((2, 0),), 3: ((2, 1),), 4: ((2, 2),),
                   5: ((2, 3),), 6: ((3, 0), (3, 1)), 7: ((3, 2), (3, 3))}
            late = {8: (U,), 9: (marks(0, 0),), 10: (marks(0, 1),), 11: (marks(0, 2),), 12: (marks(0, 3),)}
            out = [("prep", b, marks(c, t)) for c, t in own.get(m, ())]
            if b == 0:
                ahead = {8: (0, 1), 9: (2, 3), 10: (U, marks(0, 0)), 11: (marks(0, 1), marks(0, 2)),
                         12: (marks(0, 3),)}
                if 2 <= m < 2 + TT:
                    out.append(("wo", NB - 1, m - 2))
            else:
                ahead = {2: (0,), 3: (1,), 4: (2,), 5: (3,), **late}
            if b < NB - 1:
                out += [("prep", b + 1, s) for s in ahead.get(m, ())]
            return out

        ORDER = [("prep", 0, marks(0, t)) for t in range(TT)]
        ORDER += [step for b in range(NB) for m in range(MT) for step in slot_steps(b, m)]

        def w2_tile(own, late, m):
            return own[:, m] if m < W2_OWN else late[:, m - W2_OWN]

        def number(b, s, kind="prep"):
            return ORDER.index((kind, b, s)) if (kind, b, s) in ORDER else -1

        def halves(n):
            return sum(step[0] == "prep" for step in ORDER[:n + 1])

        @block.sync
        def _(sp):
            def load_x(b, t):
                i = b * TT + t
                if i >= TT + 2:
                    bb, tt = divmod(i - 2, TT)
                    sp.wait_ge(prep_mm, number(bb, tt) + 1)
                sp.dma_start(x_sb[t % 2][:], x1[i * P * D:(i + 1) * P * D].rearrange("(p d) -> p d", p=P)
                             ).then_inc(x_in[t % 2], DMA)

            def load_w2(m):
                if m >= 2:
                    sp.wait_ge(w2_low, m - 1)
                sp.dma_start(w2_raw[m % 2][:], w2[m * P:(m + 1) * P]).then_inc(w2_in[m % 2], DMA)

            def load_y(round_, src):
                if round_ > 1:
                    sp.wait_ge(out_sent, DMA * (round_ - 1))
                elif round_:
                    sp.wait_ge(x1_out, DMA)
                sp.dma_start(y[:], src.rearrange("(t p d) -> p t d", t=TT, p=P)).then_inc(y_in, DMA)

            def store(round_, dst, done):
                sp.wait_ge(out_ready, TT * (round_ + 1))
                sp.dma_start(dst.rearrange("(t p d) -> p t d", t=TT, p=P), y[:]).then_inc(done, DMA)

            flat = lambda dram, b: dram[b * S * D:(b + 1) * S * D]
            load_w2(0)
            load_w2(1)
            load_y(0, flat(x, NB - 1))
            for b in range(NB):
                for m in range(MT):
                    if b == 0 and m + 2 < MT:
                        load_w2(m + 2)
                    at = 6 if b == 0 else 0
                    if b + 1 < NB and at <= m < at + TT:
                        load_x(b + 1, m - at)
                    if b == 0 and m == 8:
                        store(0, flat(x1, NB - 1), x1_out)
                    if b == 0 and m == 10:
                        load_y(1, flat(x1, 0))
                    if b and m == 3:
                        store(b, flat(out, b - 1), out_sent)
                    if b and m == 5:
                        load_y(b + 1, flat(x1, b))
            store(NB, flat(out, NB - 1), out_sent)
            sp.wait_ge(out_sent, NB * DMA)

        @block.gpsimd
        def _(pool):
            nc.gpsimd.memset(neg_half[:], -0.5).then_inc(half_set, 1)

            def low_w2(m):
                pool.wait_ge(w2_high, m + 1)
                nc.gpsimd.tensor_tensor(w2_tile(w2_l, wo_l, m), w2_raw[m % 2][:],
                                        w2_tile(w2_h, wo_h, m).bitcast(F32), ALU.subtract).then_inc(w2_low, 1)

            def low_g(b, m):
                i = b * MT + m
                pool.wait_ge(g_high, i + 1)
                if i >= 2:
                    pool.wait_ge(out_mm, i - 1)
                nc.gpsimd.tensor_tensor(g_l[m % 2][:], picked[m % 2][:], g_h[m % 2][:].bitcast(F32),
                                        ALU.subtract).then_inc(g_ready, 1)

            def root(round_):
                pool.wait_ge(var_ready, round_ + 1)
                nc.gpsimd.tensor_tensor(rstd[:], var[:], neg_half[:], ALU.pow).then_inc(rstd_ready, 1)

            pool.wait_ge(half_set, 1)
            low_w2(0)
            for b in range(NB):
                for m in range(MT):
                    low_g(b, m)
                    if b == 0 and m + 1 < MT:
                        low_w2(m + 1)
                    if m == (1 if b else 6):
                        root(b)
            root(NB)

        @block.scalar
        def _(act):
            def turn(b, m):
                i = b * MT + m
                act.wait_ge(mask_turned, i + 1)
                if i >= 2:
                    act.wait_ge(z_done, i - 1)
                nc.scalar.activation(mask_t[m % 2][:], ps_t[:], ACT.Copy).then_inc(mask_t_ready, 1)

            def relu(b, m):
                i = b * MT + m
                act.wait_ge(h_done, i + 1)
                if i >= 2:
                    act.wait_ge(picked_ready, i - 1)
                nc.scalar.activation(act_r[m % 2][:], ps_h[:], ACT.Relu).then_inc(relu_ready, 1)

            def high_g(b, m):
                i = b * MT + m
                act.wait_ge(picked_ready, i + 1)
                if i >= 2:
                    act.wait_ge(out_mm, i - 1)
                nc.scalar.activation(g_h[m % 2][:], picked[m % 2][:], ACT.Copy).then_inc(g_high, 1)

            def high_w2(m):
                act.wait_ge(w2_in[m % 2], DMA * (m // 2 + 1))
                if m == W2_OWN:
                    act.wait_ge(prep_mm, number(NB - 1, TT - 1, "wo") + 1)
                nc.scalar.activation(w2_tile(w2_h, wo_h, m), w2_raw[m % 2][:], ACT.Copy).then_inc(w2_high, 1)

            high_w2(0)
            turn(0, 0)
            for b in range(NB):
                for m in range(MT):
                    if b == 0 and m + 1 < MT:
                        high_w2(m + 1)
                    relu(b, m)
                    if b * MT + m + 1 < NB * MT:
                        turn(*divmod(b * MT + m + 1, MT))
                    high_g(b, m)

        @block.vector
        def _(dve):
            def step(kind, b, s, bank):
                n = number(b, s, kind)
                half = halves(n)
                dve.wait_ge(prep_mm, n + 1)
                if kind == "wo":
                    if s == 0:
                        dve.wait_ge(y_in, DMA)
                    nc.vector.tensor_tensor(y[:, s], bank[:], y[:, s], ALU.add).then_inc(prep_done, 1)
                    dve.wait_ge(prep_done, n + 1)
                    nc.vector.bn_stats(stats[:, s], y[:, s]).then_inc(stat_done, 1)
                    return
                if s < TT:
                    dst = [part[b % 2][:, :, s * P:(s + 1) * P] for part in (xt_h, xt_l)]
                    src = bank[:].rearrange("p (k t) -> p k t", k=KT)
                    if s == 0 and b >= 2:
                        dve.wait_ge(h_done, MT * (b - 1))
                    elif s == 0:
                        dve.wait_ge(prep_mm, number(NB - 1, TT - 1, "wo") + 1)
                    nc.vector.tensor_copy(dst[0], src).then_inc(prep_half, 1)
                    dve.wait_ge(prep_half, half)
                    nc.vector.tensor_tensor(dst[1], src, dst[0].bitcast(F32), ALU.subtract).then_inc(prep_done, 1)
                elif s == U:
                    nc.vector.tensor_copy(u[:], bank[0:80]).then_inc(prep_half, 1)
                    dve.wait_ge(prep_half, half)
                    nc.vector.tensor_tensor(u[32:32 + RANK], bank[32:32 + RANK],
                                            u[32:32 + RANK].bitcast(F32), ALU.subtract).then_inc(prep_done, 1)
                else:
                    c, t = divmod(s - TT - 1, TT)
                    src = bank[:, 0:CH].rearrange("p (n k) -> p n k", k=BLK)
                    nc.vector.tensor_reduce(top[t % 2][:], src, AX.X, ALU.max).then_inc(prep_half, 1)
                    dve.wait_ge(prep_half, half)
                    if b and t == 0:
                        dve.wait_ge(mask_turned, MT * (b - 1) + min(MT, -(-(c + 1) * CH // P)))
                    nc.vector.tensor_tensor(
                        mask[:, t, c * CH:(c + 1) * CH].rearrange("p (n k) -> p n k", k=BLK), src,
                        top[t % 2][:].rearrange("p (n o) -> p n o", o=1).broadcast_to([P, CH // BLK, BLK]),
                        ALU.is_equal).then_inc(prep_done, 1)

            def pick(b, m):
                i = b * MT + m
                dve.wait_ge(z_done, i + 1)
                dve.wait_ge(relu_ready, i + 1)
                if i >= 2:
                    dve.wait_ge(g_ready, i - 1)
                nc.vector.scalar_tensor_tensor(picked[m % 2][:], ps_z[:], 1.0, act_r[m % 2][:], ALU.is_equal,
                                               ALU.mult).then_inc(picked_ready, 1)

            def add(b):
                dve.wait_ge(y_in, DMA * (b + 2))
                dve.wait_ge(out_mm, MT * (b + 1))
                for t in range(TT):
                    nc.vector.tensor_tensor(y[:, t], ps_out[t][:], y[:, t], ALU.add).then_inc(y_ready, 1)

            def statistics(b):
                for t in range(TT):
                    dve.wait_ge(y_ready, TT * b + t + 1)
                    nc.vector.bn_stats(stats[:, t], y[:, t]).then_inc(stat_done, 1)
                variance(b + 1)

            def variance(round_):
                for t in range(TT):
                    dve.wait_ge(stat_done, TT * round_ + t + 1)
                    nc.vector.bn_aggr(mv[:, t], stats[:, t]).then_inc(aggr_done, 1)
                dve.wait_ge(aggr_done, TT * (round_ + 1))
                nc.vector.tensor_scalar(var[:], mv[:, :, 1], EPS, None, ALU.add).then_inc(var_ready, 1)

            def norm(round_):
                dve.wait_ge(rstd_ready, round_ + 1)
                for t in range(TT):
                    nc.vector.tensor_scalar(y[:, t], y[:, t], mv[:, t, 0:1], rstd[:, t:t + 1],
                                            ALU.subtract, ALU.mult).then_inc(out_ready, 1)

            for t in range(TT):
                step("prep", 0, marks(0, t), (ps_prep, ps_z, ps_h)[t % 3])
            for b in range(NB):
                for m in range(MT):
                    steps = slot_steps(b, m)
                    if steps:
                        step(*steps[0], ps_prep)
                    pick(b, m)
                    if len(steps) > 1:
                        step(*steps[1], ps_prep)
                    if b and m == 0:
                        add(b - 1)
                    if b and m == 1:
                        statistics(b - 1)
                    if b and m == 2:
                        norm(b)
                    if b == 0 and m == 6:
                        variance(0)
                    if b == 0 and m == 7:
                        norm(0)
            add(NB - 1)
            statistics(NB - 1)
            norm(NB)

        @block.tensor
        def _(pe):
            def step(kind, b, s, bank, banks=1):
                n = number(b, s, kind)
                if n >= banks:
                    pe.wait_ge(prep_done, n - banks + 1)
                if kind == "wo":
                    for r in range(REP):
                        for i, (a, w) in enumerate(((att_h, wo_h), (att_h, wo_l), (att_l, wo_h))):
                            last = nc.tensor.matmul(bank[:], a[:, r, s * P:(s + 1) * P], w[:, r],
                                                    start=(r == 0 and i == 0), stop=(r == REP - 1 and i == 2))
                elif s < TT:
                    pe.wait_ge(x_in[s % 2], DMA * ((b - 1) * TT // 2 + s // 2 + 1))
                    for k in range(KT):
                        last = nc.tensor.transpose(bank[:, k * P:(k + 1) * P], x_sb[s % 2][:, k * P:(k + 1) * P],
                                                   ident[:])
                elif s == U:
                    pe.wait_ge(prep_done, n)
                    for k in range(KT):
                        for i, (c, xx) in enumerate(((c1_h, xt_h), (c1_l, xt_h), (c1_h, xt_l))):
                            last = nc.tensor.matmul(bank[0:80], c[:, k], xx[b % 2][:, k],
                                                    start=(k == 0 and i == 0), stop=(k == KT - 1 and i == 2))
                else:
                    c, t = divmod(s - TT - 1, TT)
                    if b:
                        pe.wait_ge(prep_done, number(b, U) + 1)
                    last = nc.tensor.matmul(bank[:, 0:CH], u[:, t * P:(t + 1) * P], c2_s[:, c * CH:(c + 1) * CH],
                                            start=True, stop=True)
                last.then_inc(prep_mm, 1)

            def turn_mask(b, m):
                i = b * MT + m
                pe.wait_ge(prep_done, number(b, marks(-(-(m + 1) * P // CH) - 1, TT - 1)) + 1)
                if i:
                    pe.wait_ge(mask_t_ready, i)
                for t in range(TT):
                    last = nc.tensor.transpose(ps_t[:, t * P:(t + 1) * P], mask[:, t, m * P:(m + 1) * P], ident16[:])
                last.then_inc(mask_turned, 1)

            def inner_up(b, m, ks):
                i = b * MT + m
                if ks[0] == 0:
                    if i:
                        pe.wait_ge(relu_ready, i)
                    if m == 0 and b:
                        pe.wait_ge(prep_done, number(b, TT - 1) + 1)
                for k in ks:
                    for n, (w, xx) in enumerate(((w1_h, xt_h), (w1_h, xt_l), (w1_l, xt_h))):
                        last = nc.tensor.matmul(ps_h[:], w[:, k, m * P:(m + 1) * P], xx[b % 2][:, k],
                                                start=(k == 0 and n == 0), stop=(k == KT - 1 and n == 2))
                if ks[-1] == KT - 1:
                    last.then_inc(h_done, 1)

            def first_marks(b, m):
                i = b * MT + m
                pe.wait_ge(mask_t_ready, i + 1)
                if i:
                    pe.wait_ge(picked_ready, i)
                nc.tensor.matmul(ps_z[:], first[:], mask_t[m % 2][:], start=True, stop=True).then_inc(z_done, 1)

            def inner_down(b, m, ts):
                i = b * MT + m
                if ts[0] == 0:
                    pe.wait_ge(g_ready, i + 1)
                    if b == 0:
                        pe.wait_ge(w2_low, m + 1)
                for t in ts:
                    if m == 0 and b:
                        pe.wait_ge(y_ready, TT * (b - 1) + t + 1)
                    for n, (g, w) in enumerate(((g_h, (w2_h, wo_h)), (g_h, (w2_l, wo_l)), (g_l, (w2_h, wo_h)))):
                        last = nc.tensor.matmul(ps_out[t][:], g[m % 2][:, t * P:(t + 1) * P], w2_tile(*w, m),
                                                start=(m == 0 and n == 0), stop=(m == MT - 1 and n == 2))
                if ts[-1] == TT - 1:
                    last.then_inc(out_mm, 1)

            for t in range(TT):
                step("prep", 0, marks(0, t), (ps_prep, ps_z, ps_h)[t % 3], 3)
            pe.wait_ge(prep_done, TT)
            turn_mask(0, 0)
            for b in range(NB):
                for m in range(MT):
                    steps = slot_steps(b, m)
                    before = divmod(b * MT + m - 1, MT)
                    inner_up(b, m, (0, 1))
                    if steps:
                        step(*steps[0], ps_prep)
                    inner_up(b, m, (2, 3))
                    first_marks(b, m)
                    if b * MT + m:
                        inner_down(*before, (0, 1))
                    if len(steps) > 1:
                        step(*steps[1], ps_prep)
                    if b * MT + m:
                        inner_down(*before, (2, 3))
                    if b * MT + m + 1 < NB * MT:
                        turn_mask(*divmod(b * MT + m + 1, MT))
            inner_down(NB - 1, MT - 1, (0, 1, 2, 3))


def _constants(nc, ident, ident16, first):
    with ExitStack() as ctx:
        step = ctx.enter_context(nc.semaphore("const_step"))
        ones = ctx.enter_context(nc.sbuf_tensor("const_f", [P, P], F32))
        block = ctx.enter_context(nc.Block())

        @block.gpsimd
        def _(pool):
            nc.gpsimd.memset(ident[:], 0.0).then_inc(step, 1)
            nc.gpsimd.memset(ones[:], 0.0).then_inc(step, 1)
            pool.wait_ge(step, 2)
            nc.gpsimd.affine_select(out=ident[:], in_=ident[:], compare_op=ALU.not_equal, fill=1.0, base=0,
                                    pattern=[[-1, P]], channel_multiplier=1).then_inc(step, 1)
            nc.gpsimd.affine_select(out=ones[:], in_=ones[:], compare_op=ALU.is_ge, fill=-2.0, base=0,
                                    pattern=[[-1, P]], channel_multiplier=1).then_inc(step, 1)
            pool.wait_ge(step, 4)
            nc.gpsimd.affine_select(out=ones[:].rearrange("p (n k) -> p n k", k=BLK),
                                    in_=ones[:].rearrange("p (n k) -> p n k", k=BLK), compare_op=ALU.is_ge,
                                    fill=0.0, base=0, pattern=[[-BLK, P // BLK], [0, BLK]],
                                    channel_multiplier=1).then_inc(step, 1)
            pool.wait_ge(step, 5)
            nc.gpsimd.affine_select(out=ones[:], in_=ones[:], compare_op=ALU.not_equal, fill=1.0, base=0,
                                    pattern=[[-1, P]], channel_multiplier=1).then_inc(step, 1)
            pool.wait_ge(step, 6)
            nc.gpsimd.tensor_copy(ident16[:], ident[:]).then_inc(step, 1)
            nc.gpsimd.tensor_copy(first[:], ones[:]).then_inc(step, 1)


def build(nc, x, xT, w_qkv, wo, c1, c2, w1, w2, out):
    dram = (_scratch(nc, "q_stacks", NU * Q_UNIT), _scratch(nc, "k_stacks", NU * K_UNIT),
            _scratch(nc, "v_halves", 2 * NB * V_HALF), _scratch(nc, "sums", NU * SUMS),
            _scratch(nc, "reciprocals", NB * NH * S))
    x1 = _scratch(nc, "after_attention", NB * S * D)
    with ExitStack() as ctx:
        sb = lambda name, shape, dt=F32: ctx.enter_context(nc.sbuf_tensor(name, shape, dt))
        ident = sb("ident", [P, P])
        ident16 = sb("ident16", [P, P], BF16)
        first = sb("first", [P, P], BF16)
        c1_h, c1_l = sb("c1_h", [P, KT, 80], F32R), sb("c1_l", [P, KT, 80], F32R)
        c2_s = sb("c2_s", [80, INTER], F32R)
        wo_h, wo_l = sb("wo_h", [P, REP, D], F32R), sb("wo_l", [P, REP, D], F32R)
        _constants(nc, ident, ident16, first)
        projection = _projection_memory(nc)
        xt_h = [sb(f"xt_h{j}", [P, KT, S], F32R) for j in range(2)]
        xt_l = [sb(f"xt_l{j}", [P, KT, S], F32R) for j in range(2)]
        u = sb("u", [80, S], F32R)
        w1_h, w1_l = sb("w1_h", [P, KT, INTER], F32R), sb("w1_l", [P, KT, INTER], F32R)
        keep = (w1_h, w1_l, c1_h, c1_l, c2_s, ident, xt_h, xt_l, u, wo_h, wo_l)
        _attend(nc, x, xT, w_qkv, wo, c1, c2, w1, dram, x1, projection, keep)
        _feed_forward(nc, x, x1, out, w2, keep, ident16, first)


def kernel(L0_attn_x, L0_attn_wq, L0_attn_wk, L0_attn_wv, L0_attn_wo, L0_ffn_c1_w, L0_ffn_c2_w, L0_ffn_w1,
           L0_ffn_w2t):
    import numpy as np
    import concourse.bacc as bacc
    from concourse.bass_utils import run_bass_kernel_spmd

    x = np.asarray(L0_attn_x).reshape(NB, S, D)
    wq = np.asarray(L0_attn_wq).reshape(D, NKV, REP, HD).transpose(0, 2, 1, 3).reshape(D, D)
    wo = np.asarray(L0_attn_wo).reshape(NKV, REP, HD, D).transpose(1, 0, 2, 3).reshape(D, D)
    arrays = {
        "x": x.reshape(-1), "xT": x.transpose(0, 2, 1),
        "w_qkv": np.concatenate([wq, np.asarray(L0_attn_wk), np.asarray(L0_attn_wv)], axis=1),
        "wo": wo, "c1": np.asarray(L0_ffn_c1_w).T, "c2": np.asarray(L0_ffn_c2_w).T,
        "w1": np.asarray(L0_ffn_w1).T, "w2": np.asarray(L0_ffn_w2t),
    }
    arrays = {name: np.ascontiguousarray(a) for name, a in arrays.items()}
    nc = bacc.Bacc("TRN2", target_bir_lowering=False, num_devices=1)
    args = [nc.dram_tensor(name, a.shape, mybir.dt.from_np(a.dtype), kind="ExternalInput").ap()
            for name, a in arrays.items()]
    out = nc.dram_tensor("out", (NB * S * D,), F32, kind="ExternalOutput").ap()
    build(nc, *args, out)
    r = run_bass_kernel_spmd(nc, [arrays], core_ids=[0])
    return r.results[0]["out"].reshape(NB, S, D)
```

```python
import concourse.bass as bass
from concourse import mybir
from contextlib import ExitStack

F32 = mybir.dt.float32
F32R = mybir.dt.float32r
BF16 = mybir.dt.bfloat16
ALU = mybir.AluOpType
ACT = mybir.ActivationFunctionType
AX = mybir.AxisListType

P = 128
NB = 4
S = 512
D = 512
NH, NKV = 32, 8
HD = D // NH
REP = NH // NKV
KT = D // P
TT = S // P
KV = NKV * HD
INTER, BLK, RANK = 1792, 32, 16
MT = INTER // P
CH = 448
NC = INTER // CH
EPS = 1e-5
DMA = 16

STACK = 3 * HD
SHIFT = STACK
ROWS = STACK + 2
VW = 2 * HD
VG = NKV // 2
Q_UNIT = 2 * 2 * HD * 2 * S
K_UNIT = STACK * S
V_HALF = P * TT * VG * VW
SUMS = P * S
NU = NB * NKV


def _scratch(nc, name, n):
    return nc.dram_tensor(name, (n,), F32, kind="Internal").ap()


def _projection_memory(nc):
    with ExitStack() as ctx:
        sb = lambda name, shape, dt=F32: ctx.enter_context(nc.sbuf_tensor(name, shape, dt))
        WQ = D + 2 * KV
        return dict(
            w_raw=sb("w_raw", [P, KT, WQ]), w_h=sb("w_h", [P, KT, WQ], F32R), w_l=sb("w_l", [P, KT, WQ], F32R),
            x_raw=[sb(f"x_raw{j}", [P, KT, S]) for j in range(2)],
            x_h=[sb(f"x_h{j}", [P, KT, S], F32R) for j in range(2)],
            x_l=[sb(f"x_l{j}", [P, KT, S], F32R) for j in range(2)],
            wo_raw=sb("wo_raw", [P, REP, D]), c1_raw=sb("c1_raw", [P, KT, 80]), c2_raw=sb("c2_raw", [80, INTER]),
            parts=[sb(f"parts{j}", [P, 2, S], F32R) for j in range(3)],
            v_rows=sb("v_rows", [P, S]), v_new=sb("v_new", [P, TT, NKV, VW]))


def _attend(nc, x, xT, w_qkv, wo, c1, c2, w1, dram, x1, projection, keep):
    qs, ks, vs, sums, rden = dram
    w1_h, w1_l, c1_h, c1_l, c2_s, ident, ident16, first, xt_h, xt_l, u, wo_h, wo_l = keep
    w_raw, w_h, w_l, x_raw, x_h, x_l, wo_raw, c1_raw, c2_raw, parts, v_rows, v_new = projection.values()
    att_h, att_l = xt_h[1], xt_l[1]
    QR = 4
    TASKS = REP + 2
    LAST = NB * TASKS
    FRONT = LAST - TASKS
    FIRST_MAXIMA = FRONT - 8
    with ExitStack() as ctx:
        sb = lambda name, shape, dt=F32: ctx.enter_context(nc.sbuf_tensor(name, shape, dt))
        sem = lambda name: ctx.enter_context(nc.semaphore(name))
        sems = lambda name, n: [sem(f"{name}{j}") for j in range(n)]
        ps = lambda name, shape: ctx.enter_context(nc.psum_tensor(name, shape, F32))
        att, inv = sb("att", [P, REP, S]), sb("inv", [P, REP, S])
        den, inv_den = sb("den", [P, P]), sb("inv_den", [P, P])
        y = sb("y", [P, TT, D])
        x_sb = [sb(f"x_sb{j}", [P, D]) for j in range(2)]
        w1_raw = [sb(f"w1_raw{j}", [P, CH]) for j in range(2)]
        probs = [sb(f"probs{j}", [P, REP, S]) for j in range(2)]
        stage = [sb(f"stage{j}", [P, S]) for j in range(2)]
        q = [sb(f"q{j}", [P, 2, S], F32R) for j in range(QR)]
        k_ = [sb(f"k{j}", [P, S], F32R) for j in range(QR)]
        v = [sb(f"v{j}", [P, TT, VG, VW]) for j in range(2)]
        neg_max = [sb(f"neg_max{j}", [P, TT, 2, 2]) for j in range(2)]
        max_parts = sb("max_parts", [P, TT, 2, 2, 2], F32R)
        shift = [sb(f"shift{j}", [8, S], F32R) for j in range(2)]
        stats, mv = sb("stats", [P, TT, 6]), sb("mv", [P, TT, 2])
        var, rstd, neg_half = sb("var", [P, TT]), sb("rstd", [P, TT]), sb("neg_half", [P, TT])
        first_f = sb("first_f", [P, P])
        ps_max = [ps(f"ps_max{j}", [P, 2, S]) for j in range(2)]
        ps_st = [ps(f"ps_st{j}", [P, S]) for j in range(2)]
        ps_pv = ps("ps_pv", [P, S])
        ps_x = ps("ps_x", [P, S])
        bank = [(*ps_st, ps_pv)[i % 3] if i < FRONT else ps_x for i in range(LAST)]

        w_in, w_high, w_split = sems("w_in", TASKS), sem("w_high"), sem("w_split")
        xt_in, x_high, x_split = [sems(f"xt_in{j}_", KT) for j in range(2)], sem("x_high"), sem("x_split")
        projected, high_out, evacuated = sem("projected"), sem("high_out"), sem("evacuated")
        constants, v_copied, v_turned = sem("constants"), sem("v_copied"), sem("v_turned")
        ones_set, part_out, v_out = sem("ones_set"), sems("part_out", 3), sem("v_out")
        pre_in, pre_zero, pre = sem("pre_in"), sem("pre_zero"), sem("pre")
        unit_in, v_in, shift_in = sems("unit_in", QR), sems("v_in", 2), sems("shift_in", QR)
        max_mm, max_red = sem("max_mm"), sem("max_red")
        max_high, max_split, max_turned, shift_ready = (sem("max_high"), sem("max_split"),
                                                        sem("max_turned"), sem("shift_ready"))
        st_mm, exp_done, pv_done, stage_ready = sem("st_mm"), sem("exp_done"), sem("pv_done"), sem("stage_ready")
        stage_out, sums_in = sems("stage_out", 2), sem("sums_in")
        rden_out, inv_in = sem("rden_out"), sem("inv_in")
        inverted, att_scaled, att_high, att_split = (sem("inverted"), sem("att_scaled"), sem("att_high"),
                                                     sem("att_split"))
        wo_done, x_in, y_ready = sem("wo_done"), sems("xr_in", 2), sem("y_ready")
        stat_done, aggr_done, var_ready, rstd_ready = (sem("stat_done"), sem("aggr_done"),
                                                       sem("var_ready"), sem("rstd_ready"))
        powers_set, x1_ready, x1_out = sem("powers_set"), sem("x1_ready"), sem("x1_out")
        w1_in, w1_high, w1_low = sems("w1_in", 2), sem("w1_high"), sem("w1_low")
        f_in, turned_mm, turned_high, turned = sem("f_in"), sem("turned_mm"), sem("turned_high"), sem("turned")
        LOADS = 6
        SHIFT_TASK = 3
        NEXT_X = {(0, 2): 1, (0, TASKS - 1): 2, (2, 3): 3}
        LATE_AT = ((0, -1), (0, 2), (1, 0), (1, 2), (2, 0), (2, 2))
        WO_AT = ((5, 0), (5, 2), (6, 0), (6, 2))
        HIGH_AT = ((3, 2), (3, 3), (4, 0), (4, 1))
        block = ctx.enter_context(nc.Block())

        def parts_out(m, j):
            return sum(2 if i % (REP + 1) == REP else 1 for i in range(m) if i % 3 == j)

        def maxima_at(b, s):
            at = 2 * (TASKS * b + s - FIRST_MAXIMA)
            end = 16 if TASKS * b + s == FRONT - 1 else at + 2
            return [divmod(i, 8) for i in range(at, end) if i >= 0]

        def score_bank(n, r):
            return ps_max[r % 2][:, 1] if n >= NU - 2 and r >= 2 else ps_st[r % 2][:]

        def columns(s):
            at = (s - 1) * P if s else D + KV
            return slice(at, at + P)

        def in_sbuf(b, s):
            return TASKS * b + (s + 1 if s > 1 or b == NB - 1 else 2 - s)

        def projections_done(eng):
            eng.wait_ge(evacuated, LAST)
            for j in range(3):
                eng.wait_ge(part_out[j], DMA * parts_out(NB * (REP + 1), j))
            eng.wait_ge(v_out, 2 * DMA * NB)
            eng.wait_ge(pre, 6)

        @block.sync
        def _(sp):
            def load_x(b, k):
                if b >= 2:
                    sp.wait_ge(x_split, KT * (b - 1))
                sp.dma_start(x_raw[b % 2][:, k], xT[b, k * P:(k + 1) * P]).then_inc(xt_in[b % 2][k], DMA)

            def store_projection(b, s):
                sp.wait_ge(evacuated, in_sbuf(b, s))
                if s == 0:
                    for f in range(2):
                        at = (2 * b + f) * V_HALF
                        sp.dma_start(vs[at:at + V_HALF].rearrange("(p k g c) -> p k g c", p=P, k=TT, g=VG),
                                     v_new[:, :, f * VG:(f + 1) * VG]).then_inc(v_out, DMA)
                    return
                s -= 1
                j = ((REP + 1) * b + s) % 3
                src = parts[j][:].bitcast(F32)
                if s < REP:
                    dst = qs[b * NKV * Q_UNIT:(b + 1) * NKV * Q_UNIT].rearrange(
                        "(p a s j t) -> a j p s t", p=P, a=2, s=2, j=2)[s % 2, s // 2]
                    sp.dma_start(dst, src).then_inc(part_out[j], DMA)
                else:
                    dst = ks[b * NKV * K_UNIT:(b + 1) * NKV * K_UNIT].rearrange("(p s t) -> p s t", p=P, s=3)
                    sp.dma_start(dst[:, 0], src[:, 0]).then_inc(part_out[j], DMA)
                    sp.dma_start(dst[:, 1:3], src).then_inc(part_out[j], DMA)

            def load_unit(n):
                j, b = n % QR, n // NKV
                if n >= QR:
                    sp.wait_ge(pv_done, TT * (n - QR + 1))
                elif n == 0:
                    sp.wait_ge(ones_set, 2 * QR + 1)
                if n % NKV == 0:
                    for i in range(3):
                        sp.wait_ge(part_out[i], DMA * parts_out((b + 1) * (REP + 1), i))
                q_src = qs[n * Q_UNIT:(n + 1) * Q_UNIT].rearrange("(d a s t) -> a s d t", d=HD, a=2, s=2)
                k_src = ks[n * K_UNIT:(n + 1) * K_UNIT].rearrange("(d s t) -> s d t", d=HD, s=3)
                for a in range(2):
                    for dst, src in ((q[j][64 * a:64 * a + 2 * HD], q_src[a]),
                                     (q[j][64 * a + 2 * HD:64 * a + STACK], q_src[a, 0]),
                                     (k_[j][64 * a:64 * a + STACK], k_src)):
                        sp.dma_start(dst.bitcast(F32), src).then_inc(unit_in[j], DMA)

            def load_v(f):
                if f >= 2:
                    sp.wait_ge(pv_done, TT * VG * (f - 1))
                sp.wait_ge(v_out, 2 * DMA * (f // 2 + 1))
                sp.dma_start(v[f % 2][:].rearrange("p k g c -> p (k g c)"),
                             vs[f * V_HALF:(f + 1) * V_HALF].rearrange("(p c) -> p c", p=P)).then_inc(v_in[f % 2], DMA)

            def send_shift(n):
                sp.wait_ge(shift_ready, n + 1)
                for a in range(2):
                    sp.dma_start(q[n % QR][64 * a + SHIFT:64 * a + SHIFT + 2].bitcast(F32),
                                 shift[n % 2][4 * a:4 * a + 4].bitcast(F32)
                                 ).then_inc(shift_in[n % QR], DMA)

            def store_unit(n):
                sp.wait_ge(stage_ready, n + 1)
                sp.dma_start(sums[n * SUMS:(n + 1) * SUMS].rearrange("(p t) -> p t", p=P), stage[n % 2][:]
                             ).then_inc(stage_out[n % 2], DMA)

            def load_sums(n):
                b, g = n // NKV, n % NKV
                if g == 0 and b:
                    sp.wait_ge(att_split, REP * b)
                sp.wait_ge(stage_out[n % 2], DMA * (n // 2 + 1))
                src = sums[n * SUMS:(n + 1) * SUMS].rearrange("(r h d t) -> h d r t", r=REP, h=2, d=HD)
                sp.dma_start(att[HD * g:HD * (g + 1)], src[0]).then_inc(sums_in, DMA)
                sp.dma_start(den[HD * g:HD * (g + 1)], src[1, 0].rearrange("r (n t) -> r n t", t=P)
                             ).then_inc(sums_in, DMA)

            def spread_reciprocals(b):
                at = b * NH * S
                sp.wait_ge(inverted, b + 1)
                sp.dma_start(rden[at:at + NH * S].rearrange("(p t) -> p t", p=P), inv_den[:]).then_inc(rden_out, DMA)
                sp.wait_ge(rden_out, DMA * (b + 1))
                sp.dma_start(inv[:].rearrange("p r t -> p (r t)"),
                             rden[at:at + NH * S].rearrange("(g o t) -> g o t", g=NKV, o=1).broadcast_to(
                                 [NKV, HD, REP * S])).then_inc(inv_in, DMA)

            def load_residual(b, t):
                i = b * TT + t
                if i >= 2:
                    sp.wait_ge(y_ready, i - 1)
                sp.dma_start(x_sb[i % 2][:], x[i * P * D:(i + 1) * P * D].rearrange("(p d) -> p d", p=P)
                             ).then_inc(x_in[i % 2], DMA)

            def store_x1(b):
                sp.wait_ge(x1_ready, TT * (b + 1))
                sp.dma_start(x1[b * S * D:(b + 1) * S * D].rearrange("(t p d) -> p t d", t=TT, p=P),
                             y[:]).then_inc(x1_out, DMA)

            def load_f():
                sp.wait_ge(att_split, REP * (NB - 1))
                sp.wait_ge(x1_out, DMA)
                sp.dma_start(att[:], x1[0:S * D].rearrange("(t p d) -> p t d", t=TT, p=P)).then_inc(f_in, DMA)

            w_v = w_qkv.rearrange("(k p) n -> p k n", p=P)
            for s in range(TASKS):
                sp.dma_start(w_raw[:, :, columns(s)], w_v[:, :, columns(s)]).then_inc(w_in[s], DMA)
                if s == 0:
                    for k in range(KT):
                        load_x(0, k)
            for k in range(KT):
                load_x(1, k)
            for k in range(KT):
                load_x(2, k)
            for b in range(NB - 1):
                for s in range(TASKS):
                    store_projection(b, s)
                    if b == NB - 2 and s == SHIFT_TASK:
                        send_shift(0)
                    if b == 1 and s in (1, 3):
                        load_unit(1 + (1, 3).index(s))
                if b == 0:
                    load_unit(0)
                if b == 1:
                    load_v(0)
                    load_v(1)
                    for k in range(KT):
                        load_x(3, k)
            for n in range(NU):
                b, g = n // NKV, n % NKV
                if n == NU - 3:
                    load_f()
                if n:
                    store_unit(n - 1)
                if n + 3 < NU:
                    load_unit(n + 3)
                if g % VG == 1 and 1 < n // VG + 1 < 2 * NB:
                    load_v(n // VG + 1)
                if n + 1 < NU:
                    send_shift(n + 1)
                for t in range(TT):
                    if b and WO_AT[t][0] == g + 1:
                        load_residual(b - 1, t)
                for t in range(TASKS):
                    if not b and LATE_AT[t][0] == g:
                        store_projection(NB - 1, t)
                if n == 4:
                    projections_done(sp)
                for i in {2: (), 3: (), 4: (n - 4, n - 3, n - 2)}.get(g, (n - 2,)):
                    if 0 <= i < NU - NKV:
                        load_sums(i)
                if b and g == 2:
                    spread_reciprocals(b - 1)
                if b > 1 and g == 0:
                    store_x1(b - 2)
            store_x1(NB - 2)
            store_unit(NU - 1)
            for j in range(2):
                sp.wait_ge(stage_out[j], NU // 2 * DMA)
            sp.wait_ge(x1_out, (NB - 1) * DMA)

        @block.gpsimd
        def _(pool):
            nc.gpsimd.memset(ident[:], 0.0).then_inc(constants, 1)
            nc.gpsimd.memset(first_f[:], 0.0).then_inc(constants, 1)
            pool.wait_ge(constants, 2)
            nc.gpsimd.affine_select(out=ident[:], in_=ident[:], compare_op=ALU.not_equal, fill=1.0, base=0,
                                    pattern=[[-1, P]], channel_multiplier=1).then_inc(constants, 1)
            nc.gpsimd.affine_select(out=first_f[:], in_=first_f[:], compare_op=ALU.is_ge, fill=-2.0, base=0,
                                    pattern=[[-1, P]], channel_multiplier=1).then_inc(constants, 1)
            pool.wait_ge(constants, 4)
            nc.gpsimd.affine_select(out=first_f[:].rearrange("p (n k) -> p n k", k=BLK),
                                    in_=first_f[:].rearrange("p (n k) -> p n k", k=BLK), compare_op=ALU.is_ge,
                                    fill=0.0, base=0, pattern=[[-BLK, P // BLK], [0, BLK]],
                                    channel_multiplier=1).then_inc(constants, 1)
            pool.wait_ge(constants, 5)
            nc.gpsimd.affine_select(out=first_f[:], in_=first_f[:], compare_op=ALU.not_equal, fill=1.0, base=0,
                                    pattern=[[-1, P]], channel_multiplier=1).then_inc(constants, 1)
            pool.wait_ge(constants, 6)
            nc.gpsimd.tensor_copy(ident16[:], ident[:]).then_inc(constants, 1)
            nc.gpsimd.tensor_copy(first[:], first_f[:]).then_inc(constants, 1)
            nc.gpsimd.memset(neg_half[:], -0.5).then_inc(powers_set, 1)
            nc.gpsimd.memset(c1_raw[:], 0.0).then_inc(pre_zero, 1)
            nc.gpsimd.memset(c2_raw[:], 0.0).then_inc(pre_zero, 1)
            pool.dma_start(wo_raw[:], wo.rearrange("(r p) n -> p r n", p=P)).then_inc(pre_in, DMA)
            pool.wait_ge(pre_zero, 2)
            for n in range(3):
                pool.dma_start(c1_raw[:, :, 32 * n:32 * n + RANK],
                               c1.rearrange("(k p) n -> p k n", p=P)).then_inc(pre_in, DMA)
                pool.dma_start(c2_raw[32 * n:32 * n + RANK, :], c2).then_inc(pre_in, DMA)
            pool.wait_ge(pre_in, 7 * DMA)
            nc.gpsimd.tensor_copy(wo_h[:], wo_raw[:]).then_inc(pre, 1)
            nc.gpsimd.tensor_copy(c1_h[:], c1_raw[:]).then_inc(pre, 1)
            nc.gpsimd.tensor_copy(c2_s[:], c2_raw[:]).then_inc(pre, 1)
            pool.wait_ge(pre, 3)
            nc.gpsimd.tensor_tensor(wo_l[:], wo_raw[:], wo_h[:].bitcast(F32), ALU.subtract).then_inc(pre, 1)
            nc.gpsimd.tensor_tensor(c1_l[:], c1_raw[:], c1_h[:].bitcast(F32), ALU.subtract).then_inc(pre, 1)
            pool.wait_ge(pre, 5)
            nc.gpsimd.tensor_tensor(c2_s[64:80], c2_raw[64:80], c2_s[64:80].bitcast(F32),
                                    ALU.subtract).then_inc(pre, 1)

            pool.wait_ge(pre, 6)
            pool.wait_ge(x_split, KT * (NB - 1))
            for k in range(KT):
                pool.wait_ge(x_high, KT * (NB - 1) + k + 1)
                nc.gpsimd.tensor_tensor(x_l[(NB - 1) % 2][:, k], x_raw[(NB - 1) % 2][:, k],
                                        x_h[(NB - 1) % 2][:, k].bitcast(F32), ALU.subtract).then_inc(x_split, 1)

            w1_v = w1.rearrange("(k p) n -> p k n", p=P)
            projections_done(pool)

            def load_w1(i):
                if i >= 2:
                    pool.wait_ge(w1_low, i - 1)
                pool.dma_start(w1_raw[i % 2][:], w1_v[:, i // NC, (i % NC) * CH:(i % NC + 1) * CH]
                               ).then_inc(w1_in[i % 2], DMA)
            load_w1(0)
            for i in range(KT * NC):
                if i + 1 < KT * NC:
                    load_w1(i + 1)
                k, c = i // NC, i % NC
                pool.wait_ge(w1_in[i % 2], DMA * (i // 2 + 1))
                nc.gpsimd.tensor_copy(w1_h[:, k, c * CH:(c + 1) * CH], w1_raw[i % 2][:]).then_inc(w1_high, 1)
                pool.wait_ge(w1_high, i + 1)
                nc.gpsimd.tensor_tensor(w1_l[:, k, c * CH:(c + 1) * CH], w1_raw[i % 2][:],
                                        w1_h[:, k, c * CH:(c + 1) * CH].bitcast(F32),
                                        ALU.subtract).then_inc(w1_low, 1)
            pool.wait_ge(powers_set, 1)
            for b in range(NB - 1):
                pool.wait_ge(inv_in, DMA * (b + 1))
                for r in range(REP):
                    nc.gpsimd.tensor_tensor(att[:, r], att[:, r], inv[:, r], ALU.mult).then_inc(att_scaled, 1)
                for r in range(REP):
                    pool.wait_ge(att_high, REP * b + r + 1)
                    nc.gpsimd.tensor_tensor(att_l[:, r], att[:, r], att_h[:, r].bitcast(F32), ALU.subtract
                                            ).then_inc(att_split, 1)
                pool.wait_ge(var_ready, b + 1)
                nc.gpsimd.tensor_tensor(rstd[:], var[:], neg_half[:], ALU.pow).then_inc(rstd_ready, 1)

        @block.scalar
        def _(act):
            def high_x(b, k):
                act.wait_ge(xt_in[b % 2][k], DMA * (b // 2 + 1))
                if b >= 2 and k == 0:
                    act.wait_ge(projected, TASKS * (b - 1))
                nc.scalar.activation(x_h[b % 2][:, k], x_raw[b % 2][:, k], ACT.Copy).then_inc(x_high, 1)

            def copy_v(b):
                act.wait_ge(projected, TASKS * b + 1)
                if b:
                    act.wait_ge(v_turned, b)
                nc.scalar.activation(v_rows[:], bank[TASKS * b][:], ACT.Copy).then_inc(v_copied, 1)

            def high_projection(b, s):
                i = TASKS * b + s
                m = (REP + 1) * b + s - 1
                act.wait_ge(projected, i + 1)
                if m >= 3:
                    act.wait_ge(part_out[m % 3], DMA * parts_out(m, m % 3))
                nc.scalar.activation(parts[m % 3][:, 0], bank[i][:], ACT.Copy).then_inc(high_out, 1)

            def turn_shift(n):
                act.wait_ge(max_turned, n + 1)
                if n >= 2:
                    act.wait_ge(shift_in[(n - 2) % QR], 2 * DMA * ((n - 2) // QR + 1))
                nc.scalar.activation(shift[n % 2][:], ps_x[0:8], ACT.Copy).then_inc(shift_ready, 1)

            def take_sums(n):
                act.wait_ge(pv_done, TT * (n + 1))
                if n >= 2:
                    act.wait_ge(stage_out[n % 2], DMA * (n // 2))
                nc.scalar.activation(stage[n % 2][:], ps_pv[:], ACT.Copy).then_inc(stage_ready, 1)

            def high_att(b, r):
                act.wait_ge(att_scaled, REP * b + r + 1)
                if b and r == 0:
                    act.wait_ge(wo_done, TT * b)
                nc.scalar.activation(att_h[:, r], att[:, r], ACT.Copy).then_inc(att_high, 1)

            for s in range(TASKS):
                act.wait_ge(w_in[s], DMA)
                nc.scalar.activation(w_h[:, :, columns(s)], w_raw[:, :, columns(s)], ACT.Copy).then_inc(w_high, 1)
                if s == 0:
                    for k in range(KT):
                        high_x(0, k)
            for b in range(NB - 1):
                copy_v(b)
                for s in range(1, TASKS):
                    high_projection(b, s)
                    if b == NB - 2 and s == SHIFT_TASK:
                        turn_shift(0)
                    if (b, s) in NEXT_X:
                        for k in range(KT):
                            high_x(NEXT_X[b, s], k)
            copy_v(NB - 1)
            for n in range(NU):
                b, g = n // NKV, n % NKV
                for kt in range(TT):
                    for r in range(REP):
                        i = (n * TT + kt) * REP + r
                        if r == 2 and not b and (g, kt) in LATE_AT[1:]:
                            high_projection(NB - 1, LATE_AT.index((g, kt)))
                        act.wait_ge(st_mm, i + 1)
                        if r == 0 and n * TT + kt >= 2:
                            act.wait_ge(pv_done, n * TT + kt - 1)
                        nc.scalar.activation(probs[kt % 2][:, r], score_bank(n, r), ACT.Exp,
                                             scale=float(HD) ** -0.5).then_inc(exp_done, 1)
                        if b and r == 2 and (g, kt) in HIGH_AT:
                            high_att(b - 1, HIGH_AT.index((g, kt)))
                    if kt == 0:
                        if n:
                            take_sums(n - 1)
                    if kt == 1 and n + 1 < NU:
                        turn_shift(n + 1)
            take_sums(NU - 1)

        @block.vector
        def _(dve):
            def low_x(b, k):
                dve.wait_ge(x_high, KT * b + k + 1)
                nc.vector.tensor_tensor(x_l[b % 2][:, k], x_raw[b % 2][:, k], x_h[b % 2][:, k].bitcast(F32),
                                        ALU.subtract).then_inc(x_split, 1)

            def row_max(n, i):
                dve.wait_ge(max_mm, 8 * n + i + 1)
                if n > 1 and i == 0:
                    dve.wait_ge(max_split, n - 1)
                nc.vector.tensor_reduce(neg_max[n % 2][:, i // 2, :, i % 2], ps_max[i % 2][:], AX.X, ALU.max,
                                        negate=True).then_inc(max_red, 1)

            def split_max(n):
                dve.wait_ge(max_red, 8 * (n + 1))
                if n:
                    dve.wait_ge(max_turned, n)
                nc.vector.tensor_copy(max_parts[:, :, :, 0], neg_max[n % 2][:]).then_inc(max_high, 1)
                dve.wait_ge(max_high, n + 1)
                nc.vector.tensor_tensor(max_parts[:, :, :, 1], neg_max[n % 2][:], max_parts[:, :, :, 0].bitcast(F32),
                                        ALU.subtract).then_inc(max_split, 1)

            def invert(b):
                dve.wait_ge(sums_in, 2 * DMA * NKV * (b + 1))
                if b:
                    dve.wait_ge(rden_out, DMA * b)
                nc.vector.reciprocal(inv_den[:], den[:]).then_inc(inverted, 1)

            def add_tile(b, t):
                i = b * TT + t
                dve.wait_ge(wo_done, i + 1)
                dve.wait_ge(x_in[i % 2], DMA * (i // 2 + 1))
                if b and t == 0:
                    dve.wait_ge(x1_out, DMA * b)
                nc.vector.tensor_tensor(y[:, t], ps_x[:], x_sb[i % 2][:], ALU.add).then_inc(y_ready, 1)
                dve.wait_ge(y_ready, i + 1)
                nc.vector.bn_stats(stats[:, t], y[:, t]).then_inc(stat_done, 1)
                dve.wait_ge(stat_done, i + 1)
                nc.vector.bn_aggr(mv[:, t], stats[:, t]).then_inc(aggr_done, 1)

            def variance(b):
                dve.wait_ge(aggr_done, TT * (b + 1))
                nc.vector.tensor_scalar(var[:], mv[:, :, 1], EPS, None, ALU.add).then_inc(var_ready, 1)

            def norm(b, t):
                dve.wait_ge(rstd_ready, b + 1)
                nc.vector.tensor_scalar(y[:, t], y[:, t], mv[:, t, 0:1], rstd[:, t:t + 1],
                                        ALU.subtract, ALU.mult).then_inc(x1_ready, 1)

            def split_x(t):
                dst = [part[0][:, :, t * P:(t + 1) * P] for part in (xt_h, xt_l)]
                src = ps_max[t % 2][:, 0].rearrange("p (k t) -> p k t", k=KT)
                dve.wait_ge(turned_mm, t + 1)
                nc.vector.tensor_copy(dst[0], src).then_inc(turned_high, 1)
                dve.wait_ge(turned_high, t + 1)
                nc.vector.tensor_tensor(dst[1], src, dst[0].bitcast(F32), ALU.subtract).then_inc(turned, 1)

            def evacuate(b, s):
                i = TASKS * b + s
                if s:
                    m = (REP + 1) * b + s - 1
                    dve.wait_ge(high_out, m + 1)
                    nc.vector.tensor_tensor(parts[m % 3][:, 1], bank[i][:], parts[m % 3][:, 0].bitcast(F32),
                                            ALU.subtract).then_inc(evacuated, 1)
                else:
                    dve.wait_ge(v_turned, b + 1)
                    if b:
                        dve.wait_ge(v_out, 2 * DMA * b)
                    nc.vector.tensor_copy(v_new[:, :, :, 0:HD],
                                          ps_x[:].rearrange("p (k g d) -> p k g d", k=TT, g=NKV)
                                          ).then_inc(evacuated, 1)

            for s in range(TASKS):
                dve.wait_ge(w_high, s + 1)
                nc.vector.tensor_tensor(w_l[:, :, columns(s)], w_raw[:, :, columns(s)],
                                        w_h[:, :, columns(s)].bitcast(F32), ALU.subtract).then_inc(w_split, 1)
                if s == 0:
                    for k in range(KT):
                        low_x(0, k)
            for j in range(QR):
                for a in range(2):
                    nc.vector.memset(k_[j][64 * a + 32:64 * a + 64].bitcast(F32), 1.0).then_inc(ones_set, 1)
            nc.vector.memset(v_new[:, :, :, HD:VW], 1.0).then_inc(ones_set, 1)
            for b in range(NB - 1):
                for s in range(TASKS):
                    if s:
                        evacuate(b, s)
                    if s == 1:
                        evacuate(b, 0)
                    for n, i in maxima_at(b, s):
                        row_max(n, i)
                        if (n, i) == (0, 7):
                            split_max(0)
                    if NEXT_X.get((b, s), NB - 1) < NB - 1:
                        for k in range(KT):
                            low_x(NEXT_X[b, s], k)
            for n in range(NU):
                b, g = n // NKV, n % NKV
                if n + 2 < NU:
                    for i in range(8):
                        row_max(n + 2, i)
                        if i == 0:
                            split_max(n + 1)
                        if not b and i % 2 == 0 and (g, i // 2) in LATE_AT[1:]:
                            evacuate(NB - 1, LATE_AT.index((g, i // 2)))
                        if not b and i % 2 == 0 and (g, i // 2 - 1) == LATE_AT[0]:
                            evacuate(NB - 1, 0)
                        if b and (g, i) == (2, 0):
                            invert(b - 1)
                        if b and i % 2 == 0 and (g, i // 2) in WO_AT:
                            add_tile(b - 1, WO_AT.index((g, i // 2)))
                        if b and g == 7 and i >= 4:
                            norm(b - 1, i - 4)
                    if n + 2 == NU - 1:
                        split_max(NU - 1)
                if b and g == 6:
                    for t in range(TT if n == NU - 2 else 0):
                        if t % 2 == 0:
                            add_tile(b - 1, 2 + t // 2)
                        split_x(t)
                    variance(b - 1)
                if n == NU - 1:
                    for t in range(TT):
                        norm(b - 1, t)
            dve.wait_ge(turned_mm, TT + 1)
            nc.vector.tensor_copy(u[:], ps_max[0][0:80, 0]).then_inc(turned_high, 1)
            dve.wait_ge(turned_high, TT + 1)
            nc.vector.tensor_tensor(u[32:32 + RANK], ps_max[0][32:32 + RANK, 0],
                                    u[32:32 + RANK].bitcast(F32), ALU.subtract).then_inc(turned, 1)

        @block.tensor
        def _(pe):
            def project(b, s):
                i = TASKS * b + s
                xs, ws = (x_h, x_h, x_l), (w_h, w_l, w_h)
                if i >= 3:
                    pe.wait_ge(evacuated, i - 2 if i < FRONT else i)
                if b == 0:
                    pe.wait_ge(w_split, s + 1)
                for k in range(KT):
                    if s == 0:
                        pe.wait_ge(x_split, KT * b + k + 1)
                    for n in range(3):
                        last = nc.tensor.matmul(bank[i][:], ws[n][:, k, columns(s)], xs[n][b % 2][:, k],
                                                start=(k == 0 and n == 0), stop=(k == KT - 1 and n == 2))
                last.then_inc(projected, 1)

            def turn_v(b):
                pe.wait_ge(v_copied, b + 1)
                if b == 0:
                    pe.wait_ge(constants, 8)
                if 0 < b < NB - 1:
                    pe.wait_ge(evacuated, in_sbuf(b - 1, 0))
                for t in range(TT):
                    last = nc.tensor.transpose(ps_x[:, t * P:(t + 1) * P], v_rows[:, t * P:(t + 1) * P], ident[:])
                last.then_inc(v_turned, 1)

            def scores(n, i, a):
                if n >= NU:
                    return
                if a == 0:
                    if i == 0:
                        pe.wait_ge(unit_in[n % QR], LOADS * DMA * (n // QR + 1))
                    if 8 * n + i >= 2:
                        pe.wait_ge(max_red, 8 * n + i - 1)
                t, j = i // 2, i % 2
                mm = nc.tensor.matmul(ps_max[i % 2][:, a], q[n % QR][64 * a:64 * a + STACK, j, t * P:(t + 1) * P],
                                      k_[n % QR][64 * a:64 * a + STACK, :], start=True, stop=True)
                if a == 1:
                    mm.then_inc(max_mm, 1)

            def turn_max(n):
                pe.wait_ge(max_split, n + 1)
                b, g = (n - 1) // NKV, (n - 1) % NKV
                tiles = TT * (b - 1) + sum(at <= (g, 1) for at in WO_AT)
                if tiles > 0:
                    pe.wait_ge(y_ready, tiles)
                elif n == 0:
                    pe.wait_ge(evacuated, in_sbuf(NB - 2, 0))
                else:
                    pe.wait_ge(evacuated, FRONT + sum(at <= (n - 1, 1) for at in LATE_AT))
                if n >= 1:
                    pe.wait_ge(shift_ready, n)
                for t in range(TT):
                    last = nc.tensor.transpose(ps_x[0:8, t * P:(t + 1) * P],
                                               max_parts[:, t].rearrange("p a h j -> p (a h j)").bitcast(F32), ident[:])
                last.then_inc(max_turned, 1)

            def scores_t(n, kt, r):
                i = (n * TT + kt) * REP + r
                if kt == 0 and r == 0:
                    pe.wait_ge(shift_in[n % QR], 2 * DMA * (n // QR + 1))
                if i < 2:
                    pe.wait_ge(evacuated, FRONT - 2 + i)
                elif n < NU - 2 or (n, kt) == (NU - 2, 0):
                    pe.wait_ge(exp_done, i - 1)
                    if r == 2 and n == NU - 2:
                        pe.wait_ge(max_red, 8 * NU)
                else:
                    pe.wait_ge(exp_done, i - 3)
                a, j = r % 2, r // 2
                nc.tensor.matmul(score_bank(n, r), k_[n % QR][64 * a:64 * a + ROWS, kt * P:(kt + 1) * P],
                                 q[n % QR][64 * a:64 * a + ROWS, j, :], start=True, stop=True).then_inc(st_mm, 1)

            def weigh(n, kt):
                f, g = n // VG, n % VG
                pe.wait_ge(exp_done, (n * TT + kt + 1) * REP)
                if kt == 0 and n:
                    pe.wait_ge(stage_ready, n)
                elif kt == 0:
                    pe.wait_ge(evacuated, FRONT)
                if kt == 0 and g == 0:
                    pe.wait_ge(v_in[f % 2], DMA * (f // 2 + 1))
                for r in range(REP):
                    last = nc.tensor.matmul(ps_pv[32 * r:32 * r + VW], v[f % 2][:, kt, g], probs[kt % 2][:, r],
                                            start=(kt == 0), stop=(kt == TT - 1))
                last.then_inc(pv_done, 1)

            def project_out(b, t, turns):
                i = b * TT + t
                if t == 0:
                    pe.wait_ge(att_split, REP * (b + 1))
                    if b == 0:
                        pe.wait_ge(pre, 6)
                if i:
                    pe.wait_ge(y_ready, i)
                pe.wait_ge(shift_ready, turns)
                for r in range(REP):
                    for n, (a, w) in enumerate(((att_h, wo_h), (att_h, wo_l), (att_l, wo_h))):
                        last = nc.tensor.matmul(ps_x[:], a[:, r, t * P:(t + 1) * P], w[:, r],
                                                start=(r == 0 and n == 0), stop=(r == REP - 1 and n == 2))
                last.then_inc(wo_done, 1)

            def turn_x(t):
                pe.wait_ge(f_in, DMA)
                if t >= 2:
                    pe.wait_ge(turned, t - 1)
                elif t == 0:
                    pe.wait_ge(max_red, 8 * NU)
                for k in range(KT):
                    last = nc.tensor.transpose(ps_max[t % 2][:, 0, k * P:(k + 1) * P], att[:, t, k * P:(k + 1) * P],
                                               ident[:])
                last.then_inc(turned_mm, 1)

            def first_u():
                pe.wait_ge(turned, TT)
                for k in range(KT):
                    for i, (c, xx) in enumerate(((c1_h, xt_h), (c1_l, xt_h), (c1_h, xt_l))):
                        last = nc.tensor.matmul(ps_max[0][0:80, 0], c[:, k], xx[0][:, k],
                                                start=(k == 0 and i == 0), stop=(k == KT - 1 and i == 2))
                last.then_inc(turned_mm, 1)

            for b in range(NB - 1):
                for s in range(TASKS):
                    project(b, s)
                    if s == 1:
                        turn_v(b)
                    for n, i in maxima_at(b, s):
                        scores(n, i, 0)
                        scores(n, i, 1)
                        if (n, i) == (1, 0):
                            turn_max(0)
            pe.wait_ge(shift_ready, 1)
            project(NB - 1, 0)
            for n in range(NU):
                b, g = n // NKV, n % NKV
                for kt in range(TT):
                    scores_t(n, kt, 0)
                    if n == 0 and kt == 0:
                        scores(2, 0, 0)
                    scores(n + 2, 2 * kt, 1)
                    scores_t(n, kt, 1)
                    if kt or n:
                        weigh(*divmod(n * TT + kt - 1, TT))
                    if not b and (g, kt - 1) == LATE_AT[0]:
                        turn_v(NB - 1)
                    if not b and (g, kt) in LATE_AT:
                        pe.wait_ge(shift_ready, n + 1 + (kt > 1))
                        project(NB - 1, LATE_AT.index((g, kt)))
                    if b and (g, kt) in WO_AT and n < NU - 2:
                        project_out(b - 1, WO_AT.index((g, kt)), n + 1 + (kt > 1))
                    scores_t(n, kt, 2)
                    scores(n + 2, 2 * kt + 1, 0)
                    scores_t(n, kt, 3)
                    scores(n + 2, 2 * kt + 1, 1)
                    scores(*divmod(8 * (n + 2) + 2 * kt + 2, 8), 0)
                    if n == NU - 2 and (g, kt) in WO_AT:
                        project_out(b - 1, WO_AT.index((g, kt)), n + 1 + (kt > 1))
                    if n == NU - 2:
                        turn_x(kt)
                    if (n, kt) == (NU - 1, 1):
                        first_u()
                    if kt == 1 and n + 1 < NU:
                        turn_max(n + 1)
            weigh(NU - 1, TT - 1)


def _feed_forward(nc, x, x1, out, w2, sums, rden, keep):
    w1_h, w1_l, c1_h, c1_l, c2_s, ident, ident16, first, xt_h, xt_l, u, wo_h, wo_l = keep
    att_h, att_l = xt_h[1], xt_l[1]
    U = TT
    W2_OWN = MT - REP
    marks = lambda c, t: TT + 1 + c * TT + t
    with ExitStack() as ctx:
        sb = lambda name, shape, dt=F32: ctx.enter_context(nc.sbuf_tensor(name, shape, dt))
        sem = lambda name: ctx.enter_context(nc.semaphore(name))
        ps = lambda name, shape, dt=F32: ctx.enter_context(nc.psum_tensor(name, shape, dt))
        w2_h = sb("w2_h", [P, W2_OWN, D], F32R)
        w2_l = sb("w2_l", [P, W2_OWN, D], F32R)
        att, inv = (w[:, W2_OWN - REP:W2_OWN].bitcast(F32) for w in (w2_h, w2_l))
        den, inv_den = sb("den_last", [P, P]), sb("inv_den_last", [P, P])
        w2_raw = [sb(f"w2_raw{j}", [P, D]) for j in range(2)]
        x_sb = [sb(f"xf_sb{j}", [P, D]) for j in range(2)]
        top = [sb(f"top{j}", [P, CH // BLK]) for j in range(2)]
        mask = sb("mask", [P, TT, INTER], BF16)
        mask_t = [sb(f"mask_t{j}", [P, S], BF16) for j in range(2)]
        act_r = [sb(f"relu{j}", [P, S]) for j in range(2)]
        picked = [sb(f"picked{j}", [P, S]) for j in range(2)]
        g_h = [sb(f"g_h{j}", [P, S], F32R) for j in range(2)]
        g_l = [sb(f"g_l{j}", [P, S], F32R) for j in range(2)]
        y = sb("yf", [P, TT, D])
        stats = sb("statsf", [P, TT, 6])
        mv = sb("mvf", [P, TT, 2])
        var = sb("varf", [P, TT])
        rstd = sb("rstdf", [P, TT])
        neg_half = sb("neg_halff", [P, TT])
        ps_out = [ps(f"ps_out{t}", [P, D]) for t in range(TT)]
        ps_h, ps_z, ps_prep = ps("ps_h", [P, S]), ps("ps_z", [P, S]), ps("ps_prep", [P, S])
        ps_t = ps("ps_t", [P, S], BF16)

        x_in = [sem(f"xf_in{j}") for j in range(2)]
        prep_mm, prep_half, prep_done = sem("prep_mm"), sem("prep_half"), sem("prep_done")
        mask_turned, mask_t_ready = sem("mask_turned"), sem("mask_t_ready")
        h_done, relu_ready, z_done, picked_ready = (sem("h_done"), sem("relu_ready"), sem("z_done"),
                                                    sem("picked_ready"))
        g_high, g_ready, out_mm = sem("g_high"), sem("g_ready"), sem("out_mm")
        w2_in, w2_high, w2_low = [sem("w2_in0"), sem("w2_in1")], sem("w2_high"), sem("w2_low")
        y_in, y_ready, stat_done, aggr_done = sem("yf_in"), sem("yf_ready"), sem("statf_done"), sem("aggrf_done")
        half_set, var_ready, rstd_ready = sem("halff_set"), sem("varf_ready"), sem("rstdf_ready")
        x1_out, last_mm = sem("x1f_out"), sem("last_mm")
        den_in, inverted, rden_out, inv_in = sem("den_in"), sem("invertedf"), sem("rdenf_out"), sem("invf_in")
        att_in, att_scaled, att_high, att_split = (sem("att_in"), sem("attf_scaled"), sem("attf_high"),
                                                   sem("attf_split"))
        out_ready, out_sent = sem("out_ready"), sem("out_sent")
        block = ctx.enter_context(nc.Block())

        def slot_steps(b, m):
            own = {0: ((1, 0), (1, 1)), 1: ((1, 2), (1, 3)), 2: ((2, 0),), 3: ((2, 1),), 4: ((2, 2),),
                   5: ((2, 3),), 6: ((3, 0), (3, 1)), 7: ((3, 2), (3, 3))}
            if b == 0:
                own.update({6: ((3, 0),), 7: ((3, 1),), 8: ((3, 2), (3, 3))})
            late = {8: (U,), 9: (marks(0, 0),), 10: (marks(0, 1),), 11: (marks(0, 2),), 12: (marks(0, 3),)}
            out = [("prep", b, marks(c, t)) for c, t in own.get(m, ())]
            if b == 0:
                ahead = {9: (0, 1), 10: (2, 3), 11: (U, marks(0, 0)), 12: (marks(0, 1), marks(0, 2)),
                         13: (marks(0, 3),)}
                if 4 <= m < 4 + TT:
                    out.append(("wo", NB - 1, m - 4))
            else:
                ahead = {2: (0,), 3: (1,), 4: (2,), 5: (3,), **late}
            if b < NB - 1:
                out += [("prep", b + 1, s) for s in ahead.get(m, ())]
            return out

        ORDER = [("prep", 0, marks(0, t)) for t in range(TT)]
        ORDER += [step for b in range(NB) for m in range(MT) for step in slot_steps(b, m)]

        def w2_tile(own, late, m):
            return own[:, m] if m < W2_OWN else late[:, m - W2_OWN]

        def number(b, s, kind="prep"):
            return ORDER.index((kind, b, s)) if (kind, b, s) in ORDER else -1

        def halves(n):
            return sum(step[0] == "prep" for step in ORDER[:n + 1])

        @block.sync
        def _(sp):
            def load_x(b, t):
                i = b * TT + t
                if i >= TT + 2:
                    bb, tt = divmod(i - 2, TT)
                    sp.wait_ge(prep_mm, number(bb, tt) + 1)
                sp.dma_start(x_sb[t % 2][:], x1[i * P * D:(i + 1) * P * D].rearrange("(p d) -> p d", p=P)
                             ).then_inc(x_in[t % 2], DMA)

            def load_w2(m):
                if m >= 2:
                    sp.wait_ge(w2_low, m - 1)
                sp.dma_start(w2_raw[m % 2][:], w2[m * P:(m + 1) * P]).then_inc(w2_in[m % 2], DMA)

            def load_y(round_, src):
                if round_ > 1:
                    sp.wait_ge(out_sent, DMA * (round_ - 1))
                elif round_:
                    sp.wait_ge(x1_out, DMA)
                else:
                    sp.wait_ge(att_split, REP)
                sp.dma_start(y[:], src.rearrange("(t p d) -> p t d", t=TT, p=P)).then_inc(y_in, DMA)

            def store(round_, dst, done):
                sp.wait_ge(out_ready, TT * (round_ + 1))
                sp.dma_start(dst.rearrange("(t p d) -> p t d", t=TT, p=P), y[:]).then_inc(done, DMA)

            flat = lambda dram, b: dram[b * S * D:(b + 1) * S * D]
            last = sums[(NU - NKV) * SUMS:NU * SUMS]
            sp.dma_start(den[:], last.rearrange("(n h d q t) -> n h d q t", n=NH, h=2, d=HD, t=P)[:, 1, 0]
                         ).then_inc(den_in, DMA)
            load_w2(0)
            load_w2(1)
            for r in range(REP):
                sp.dma_start(att[:, r], last.rearrange("(g r h d t) -> r h g d t", r=REP, g=NKV, h=2, d=HD)[r, 0]
                             ).then_inc(att_in, DMA)
            at = (NB - 1) * NH * S
            sp.wait_ge(inverted, 1)
            sp.dma_start(rden[at:at + NH * S].rearrange("(p t) -> p t", p=P), inv_den[:]).then_inc(rden_out, DMA)
            sp.wait_ge(rden_out, DMA)
            sp.dma_start(inv.rearrange("p r t -> p (r t)"),
                         rden[at:at + NH * S].rearrange("(g o t) -> g o t", g=NKV, o=1).broadcast_to(
                             [NKV, HD, REP * S])).then_inc(inv_in, DMA)
            for b in range(NB):
                for m in range(MT):
                    if b == 0 and m == 3:
                        load_y(0, flat(x, NB - 1))
                    at = 7 if b == 0 else 0
                    if b + 1 < NB and at <= m < at + TT:
                        load_x(b + 1, m - at)
                    if b == 0 and m + 2 < MT:
                        load_w2(m + 2)
                    if b == 0 and m == 10:
                        store(0, flat(x1, NB - 1), x1_out)
                    if b == 0 and m == 12:
                        load_y(1, flat(x1, 0))
                    if b and m == 3:
                        store(b, flat(out, b - 1), out_sent)
                    if b and m == 5:
                        load_y(b + 1, flat(x1, b))
            for t in range(TT):
                sp.wait_ge(out_ready, TT * NB + t + 1)
                at = ((NB - 1) * TT + t) * P * D
                sp.dma_start(out[at:at + P * D].rearrange("(p d) -> p d", p=P), y[:, t]).then_inc(out_sent, DMA)
            sp.wait_ge(out_sent, (NB - 1 + TT) * DMA)

        @block.gpsimd
        def _(pool):
            nc.gpsimd.memset(neg_half[:], -0.5).then_inc(half_set, 1)

            def low_w2(m):
                pool.wait_ge(w2_high, m + 1)
                nc.gpsimd.tensor_tensor(w2_tile(w2_l, wo_l, m), w2_raw[m % 2][:],
                                        w2_tile(w2_h, wo_h, m).bitcast(F32), ALU.subtract).then_inc(w2_low, 1)

            def low_g(b, m):
                i = b * MT + m
                pool.wait_ge(g_high, i + 1)
                if i >= 2:
                    pool.wait_ge(out_mm, i - 1)
                nc.gpsimd.tensor_tensor(g_l[m % 2][:], picked[m % 2][:], g_h[m % 2][:].bitcast(F32),
                                        ALU.subtract).then_inc(g_ready, 1)

            def root(round_):
                pool.wait_ge(var_ready, round_ + 1)
                nc.gpsimd.tensor_tensor(rstd[:], var[:], neg_half[:], ALU.pow).then_inc(rstd_ready, 1)

            pool.wait_ge(half_set, 1)
            low_w2(0)
            for b in range(NB):
                for m in range(MT):
                    low_g(b, m)
                    if b == 0 and m + 1 < MT:
                        low_w2(m + 1)
                    if m == (1 if b else 8):
                        root(b)
            root(NB)

        @block.scalar
        def _(act):
            def turn(b, m):
                i = b * MT + m
                act.wait_ge(mask_turned, i + 1)
                if i >= 2:
                    act.wait_ge(z_done, i - 1)
                nc.scalar.activation(mask_t[m % 2][:], ps_t[:], ACT.Copy).then_inc(mask_t_ready, 1)

            def relu(b, m):
                i = b * MT + m
                act.wait_ge(h_done, i + 1)
                if i >= 2:
                    act.wait_ge(picked_ready, i - 1)
                nc.scalar.activation(act_r[m % 2][:], ps_h[:], ACT.Relu).then_inc(relu_ready, 1)

            def high_g(b, m):
                i = b * MT + m
                act.wait_ge(picked_ready, i + 1)
                if i >= 2:
                    act.wait_ge(out_mm, i - 1)
                nc.scalar.activation(g_h[m % 2][:], picked[m % 2][:], ACT.Copy).then_inc(g_high, 1)

            def high_w2(m):
                act.wait_ge(w2_in[m % 2], DMA * (m // 2 + 1))
                if m == W2_OWN - REP:
                    act.wait_ge(att_scaled, REP)
                if m == W2_OWN:
                    act.wait_ge(prep_mm, number(NB - 1, TT - 1, "wo") + 1)
                nc.scalar.activation(w2_tile(w2_h, wo_h, m), w2_raw[m % 2][:], ACT.Copy).then_inc(w2_high, 1)

            turn(0, 0)
            high_w2(0)
            for b in range(NB):
                for m in range(MT):
                    if b == 0 and m + 1 < MT:
                        high_w2(m + 1)
                    relu(b, m)
                    if b * MT + m + 1 < NB * MT:
                        turn(*divmod(b * MT + m + 1, MT))
                    high_g(b, m)
                    if (b, m) == (0, 2):
                        for r in range(REP):
                            act.wait_ge(att_scaled, r + 1)
                            nc.scalar.activation(att_h[:, r], y[:, r], ACT.Copy).then_inc(att_high, 1)

        @block.vector
        def _(dve):
            def step(kind, b, s, bank):
                n = number(b, s, kind)
                half = halves(n)
                dve.wait_ge(prep_mm, n + 1)
                if kind == "wo":
                    if s == 0:
                        dve.wait_ge(y_in, DMA)
                    nc.vector.tensor_tensor(y[:, s], bank[:], y[:, s], ALU.add).then_inc(prep_done, 1)
                    dve.wait_ge(prep_done, n + 1)
                    nc.vector.bn_stats(stats[:, s], y[:, s]).then_inc(stat_done, 1)
                    return
                if s < TT:
                    dst = [part[b % 2][:, :, s * P:(s + 1) * P] for part in (xt_h, xt_l)]
                    src = bank[:].rearrange("p (k t) -> p k t", k=KT)
                    if s == 0 and b >= 2:
                        dve.wait_ge(h_done, MT * (b - 1))
                    elif s == 0:
                        dve.wait_ge(prep_mm, number(NB - 1, TT - 1, "wo") + 1)
                    nc.vector.tensor_copy(dst[0], src).then_inc(prep_half, 1)
                    dve.wait_ge(prep_half, half)
                    nc.vector.tensor_tensor(dst[1], src, dst[0].bitcast(F32), ALU.subtract).then_inc(prep_done, 1)
                elif s == U:
                    nc.vector.tensor_copy(u[:], bank[0:80]).then_inc(prep_half, 1)
                    dve.wait_ge(prep_half, half)
                    nc.vector.tensor_tensor(u[32:32 + RANK], bank[32:32 + RANK],
                                            u[32:32 + RANK].bitcast(F32), ALU.subtract).then_inc(prep_done, 1)
                else:
                    c, t = divmod(s - TT - 1, TT)
                    src = bank[:, 0:CH].rearrange("p (n k) -> p n k", k=BLK)
                    nc.vector.tensor_reduce(top[t % 2][:], src, AX.X, ALU.max).then_inc(prep_half, 1)
                    dve.wait_ge(prep_half, half)
                    if b and t == 0:
                        dve.wait_ge(mask_turned, MT * (b - 1) + min(MT, -(-(c + 1) * CH // P)))
                    nc.vector.tensor_tensor(
                        mask[:, t, c * CH:(c + 1) * CH].rearrange("p (n k) -> p n k", k=BLK), src,
                        top[t % 2][:].rearrange("p (n o) -> p n o", o=1).broadcast_to([P, CH // BLK, BLK]),
                        ALU.is_equal).then_inc(prep_done, 1)

            def pick(b, m):
                i = b * MT + m
                dve.wait_ge(z_done, i + 1)
                dve.wait_ge(relu_ready, i + 1)
                if i >= 2:
                    dve.wait_ge(g_ready, i - 1)
                nc.vector.scalar_tensor_tensor(picked[m % 2][:], ps_z[:], 1.0, act_r[m % 2][:], ALU.is_equal,
                                               ALU.mult).then_inc(picked_ready, 1)

            def add(b):
                dve.wait_ge(y_in, DMA * (b + 2))
                dve.wait_ge(out_mm, MT * (b + 1))
                for t in range(TT):
                    nc.vector.tensor_tensor(y[:, t], ps_out[t][:], y[:, t], ALU.add).then_inc(y_ready, 1)

            def statistics(b):
                for t in range(TT):
                    dve.wait_ge(y_ready, TT * b + t + 1)
                    nc.vector.bn_stats(stats[:, t], y[:, t]).then_inc(stat_done, 1)
                variance(b + 1)

            def variance(round_):
                for t in range(TT):
                    dve.wait_ge(stat_done, TT * round_ + t + 1)
                    nc.vector.bn_aggr(mv[:, t], stats[:, t]).then_inc(aggr_done, 1)
                dve.wait_ge(aggr_done, TT * (round_ + 1))
                nc.vector.tensor_scalar(var[:], mv[:, :, 1], EPS, None, ALU.add).then_inc(var_ready, 1)

            def norm(round_):
                dve.wait_ge(rstd_ready, round_ + 1)
                for t in range(TT):
                    nc.vector.tensor_scalar(y[:, t], y[:, t], mv[:, t, 0:1], rstd[:, t:t + 1],
                                            ALU.subtract, ALU.mult).then_inc(out_ready, 1)

            for t in range(TT):
                step("prep", 0, marks(0, t), (ps_prep, ps_z)[t % 2])
                if t == 1:
                    dve.wait_ge(den_in, DMA)
                    nc.vector.reciprocal(inv_den[:], den[:]).then_inc(inverted, 1)
            for b in range(NB):
                for m in range(MT):
                    steps = slot_steps(b, m)
                    if steps:
                        step(*steps[0], ps_prep)
                    pick(b, m)
                    if len(steps) > 1:
                        step(*steps[1], ps_prep)
                    if b and m == 0:
                        add(b - 1)
                    if b and m == 1:
                        statistics(b - 1)
                    if b and m == 2:
                        norm(b)
                    if (b, m) == (0, 2):
                        dve.wait_ge(att_in, REP * DMA)
                        dve.wait_ge(inv_in, DMA)
                        for r in range(REP):
                            nc.vector.tensor_tensor(y[:, r], att[:, r], inv[:, r], ALU.mult).then_inc(att_scaled, 1)
                    if (b, m) == (0, 3):
                        for r in range(REP):
                            dve.wait_ge(att_high, r + 1)
                            nc.vector.tensor_tensor(att_l[:, r], y[:, r], att_h[:, r].bitcast(F32), ALU.subtract
                                                    ).then_inc(att_split, 1)
                    if (b, m) == (0, 8):
                        variance(0)
                    if (b, m) == (0, 9):
                        norm(0)
            dve.wait_ge(y_in, DMA * (NB + 1))
            for t in range(TT):
                dve.wait_ge(last_mm, t + 1)
                nc.vector.tensor_tensor(y[:, t], ps_out[t][:], y[:, t], ALU.add).then_inc(y_ready, 1)
                dve.wait_ge(y_ready, TT * (NB - 1) + t + 1)
                nc.vector.bn_stats(stats[:, t], y[:, t]).then_inc(stat_done, 1)
            variance(NB)
            norm(NB)

        @block.tensor
        def _(pe):
            def step(kind, b, s, bank, banks=1):
                n = number(b, s, kind)
                if n >= banks:
                    pe.wait_ge(prep_done, n - banks + 1)
                if kind == "wo":
                    if s == 0:
                        pe.wait_ge(att_split, REP)
                    for r in range(REP):
                        for i, (a, w) in enumerate(((att_h, wo_h), (att_h, wo_l), (att_l, wo_h))):
                            last = nc.tensor.matmul(bank[:], a[:, r, s * P:(s + 1) * P], w[:, r],
                                                    start=(r == 0 and i == 0), stop=(r == REP - 1 and i == 2))
                elif s < TT:
                    pe.wait_ge(x_in[s % 2], DMA * ((b - 1) * TT // 2 + s // 2 + 1))
                    for k in range(KT):
                        last = nc.tensor.transpose(bank[:, k * P:(k + 1) * P], x_sb[s % 2][:, k * P:(k + 1) * P],
                                                   ident[:])
                elif s == U:
                    pe.wait_ge(prep_done, n)
                    for k in range(KT):
                        for i, (c, xx) in enumerate(((c1_h, xt_h), (c1_l, xt_h), (c1_h, xt_l))):
                            last = nc.tensor.matmul(bank[0:80], c[:, k], xx[b % 2][:, k],
                                                    start=(k == 0 and i == 0), stop=(k == KT - 1 and i == 2))
                else:
                    c, t = divmod(s - TT - 1, TT)
                    if b:
                        pe.wait_ge(prep_done, number(b, U) + 1)
                    last = nc.tensor.matmul(bank[:, 0:CH], u[:, t * P:(t + 1) * P], c2_s[:, c * CH:(c + 1) * CH],
                                            start=True, stop=True)
                last.then_inc(prep_mm, 1)

            def turn_mask(b, m):
                i = b * MT + m
                pe.wait_ge(prep_done, number(b, marks(-(-(m + 1) * P // CH) - 1, TT - 1)) + 1)
                if i:
                    pe.wait_ge(mask_t_ready, i)
                for t in range(TT):
                    last = nc.tensor.transpose(ps_t[:, t * P:(t + 1) * P], mask[:, t, m * P:(m + 1) * P], ident16[:])
                last.then_inc(mask_turned, 1)

            def inner_up(b, m, ks):
                i = b * MT + m
                if ks[0] == 0:
                    if i:
                        pe.wait_ge(relu_ready, i)
                    if m == 0 and b:
                        pe.wait_ge(prep_done, number(b, TT - 1) + 1)
                for k in ks:
                    for n, (w, xx) in enumerate(((w1_h, xt_h), (w1_h, xt_l), (w1_l, xt_h))):
                        last = nc.tensor.matmul(ps_h[:], w[:, k, m * P:(m + 1) * P], xx[b % 2][:, k],
                                                start=(k == 0 and n == 0), stop=(k == KT - 1 and n == 2))
                if ks[-1] == KT - 1:
                    last.then_inc(h_done, 1)

            def first_marks(b, m):
                i = b * MT + m
                pe.wait_ge(mask_t_ready, i + 1)
                if i:
                    pe.wait_ge(picked_ready, i)
                nc.tensor.matmul(ps_z[:], first[:], mask_t[m % 2][:], start=True, stop=True).then_inc(z_done, 1)

            def inner_down(b, m, ts):
                i = b * MT + m
                if ts[0] == 0:
                    pe.wait_ge(g_ready, i + 1)
                    if b == 0:
                        pe.wait_ge(w2_low, m + 1)
                for t in ts:
                    if m == 0 and b:
                        pe.wait_ge(y_ready, TT * (b - 1) + t + 1)
                    for n, (g, w) in enumerate(((g_h, (w2_h, wo_h)), (g_h, (w2_l, wo_l)), (g_l, (w2_h, wo_h)))):
                        last = nc.tensor.matmul(ps_out[t][:], g[m % 2][:, t * P:(t + 1) * P], w2_tile(*w, m),
                                                start=(m == 0 and n == 0), stop=(m == MT - 1 and n == 2))
                    if i == NB * MT - 1:
                        last.then_inc(last_mm, 1)
                if ts[-1] == TT - 1 and i < NB * MT - 1:
                    last.then_inc(out_mm, 1)

            for t in range(TT):
                step("prep", 0, marks(0, t), (ps_prep, ps_z)[t % 2], 2)
                if t % 2:
                    inner_up(0, 0, (t - 1, t))
            pe.wait_ge(prep_done, TT)
            turn_mask(0, 0)
            for b in range(NB):
                for m in range(MT):
                    steps = slot_steps(b, m)
                    before = divmod(b * MT + m - 1, MT)
                    if b * MT + m:
                        inner_up(b, m, (0, 1))
                    if steps:
                        step(*steps[0], ps_prep)
                    if b * MT + m:
                        inner_up(b, m, (2, 3))
                    first_marks(b, m)
                    if b * MT + m:
                        inner_down(*before, (0, 1))
                    if len(steps) > 1:
                        step(*steps[1], ps_prep)
                    if b * MT + m:
                        inner_down(*before, (2, 3))
                    if b * MT + m + 1 < NB * MT:
                        turn_mask(*divmod(b * MT + m + 1, MT))
            inner_down(NB - 1, MT - 1, (0, 1, 2, 3))


def build(nc, x, xT, w_qkv, wo, c1, c2, w1, w2, out):
    dram = (_scratch(nc, "q_stacks", NU * Q_UNIT), _scratch(nc, "k_stacks", NU * K_UNIT),
            _scratch(nc, "v_halves", 2 * NB * V_HALF), _scratch(nc, "sums", NU * SUMS),
            _scratch(nc, "reciprocals", NB * NH * S))
    x1 = _scratch(nc, "after_attention", NB * S * D)
    with ExitStack() as ctx:
        sb = lambda name, shape, dt=F32: ctx.enter_context(nc.sbuf_tensor(name, shape, dt))
        ident = sb("ident", [P, P])
        ident16 = sb("ident16", [P, P], BF16)
        first = sb("first", [P, P], BF16)
        c1_h, c1_l = sb("c1_h", [P, KT, 80], F32R), sb("c1_l", [P, KT, 80], F32R)
        c2_s = sb("c2_s", [80, INTER], F32R)
        wo_h, wo_l = sb("wo_h", [P, REP, D], F32R), sb("wo_l", [P, REP, D], F32R)
        projection = _projection_memory(nc)
        xt_h = [sb(f"xt_h{j}", [P, KT, S], F32R) for j in range(2)]
        xt_l = [sb(f"xt_l{j}", [P, KT, S], F32R) for j in range(2)]
        u = sb("u", [80, S], F32R)
        w1_h, w1_l = sb("w1_h", [P, KT, INTER], F32R), sb("w1_l", [P, KT, INTER], F32R)
        keep = (w1_h, w1_l, c1_h, c1_l, c2_s, ident, ident16, first, xt_h, xt_l, u, wo_h, wo_l)
        _attend(nc, x, xT, w_qkv, wo, c1, c2, w1, dram, x1, projection, keep)
        _feed_forward(nc, x, x1, out, w2, *dram[3:], keep)


def kernel(L0_attn_x, L0_attn_wq, L0_attn_wk, L0_attn_wv, L0_attn_wo, L0_ffn_c1_w, L0_ffn_c2_w, L0_ffn_w1,
           L0_ffn_w2t):
    import numpy as np
    import concourse.bacc as bacc
    from concourse.bass_utils import run_bass_kernel_spmd

    x = np.asarray(L0_attn_x).reshape(NB, S, D)
    wq = np.asarray(L0_attn_wq).reshape(D, NKV, REP, HD).transpose(0, 2, 1, 3).reshape(D, D)
    wo = np.asarray(L0_attn_wo).reshape(NKV, REP, HD, D).transpose(1, 0, 2, 3).reshape(D, D)
    arrays = {
        "x": x.reshape(-1), "xT": x.transpose(0, 2, 1),
        "w_qkv": np.concatenate([wq, np.asarray(L0_attn_wk), np.asarray(L0_attn_wv)], axis=1),
        "wo": wo, "c1": np.asarray(L0_ffn_c1_w).T, "c2": np.asarray(L0_ffn_c2_w).T,
        "w1": np.asarray(L0_ffn_w1).T, "w2": np.asarray(L0_ffn_w2t),
    }
    arrays = {name: np.ascontiguousarray(a) for name, a in arrays.items()}
    nc = bacc.Bacc("TRN2", target_bir_lowering=False, num_devices=1)
    args = [nc.dram_tensor(name, a.shape, mybir.dt.from_np(a.dtype), kind="ExternalInput").ap()
            for name, a in arrays.items()]
    out = nc.dram_tensor("out", (NB * S * D,), F32, kind="ExternalOutput").ap()
    build(nc, *args, out)
    r = run_bass_kernel_spmd(nc, [arrays], core_ids=[0])
    return r.results[0]["out"].reshape(NB, S, D)
```
